# Optimizing a Trainium2 kernel written in Bass

```python
import numpy as np
import jax
import jax.numpy as jnp

def _softmax(x, axis=-1):
    return jax.nn.softmax(x, axis=axis)

def _gelu(x):
    return jax.nn.gelu(x, approximate=True)

def _silu(x):
    return jax.nn.silu(x)

def _sigmoid(x):
    return jax.nn.sigmoid(x)

def _layernorm(x, axis=-1, eps=1e-05):
    m = jnp.mean(x, axis=axis, keepdims=True)
    v = jnp.var(x, axis=axis, keepdims=True)
    return (x - m) / jnp.sqrt(v + eps)

def _scatter_add(tgt, idx, src, axis=0):
    return tgt.at[idx].add(src)

def _segment_sum(src, seg, n):
    return jax.ops.segment_sum(src, seg, n)
kernel_name = 'mk_recurrent_d1_jaxref_r4_b219f5'

def setup_inputs(seed: int=0):
    np.random.seed(seed)
    _w = jnp.asarray

    def _L0_attn_setup():
        import jax, jax.numpy as jnp
        import numpy as np
        BASE_THETA = 0.5
        K_DOP = 0.2
        K_NOR = 0.15
        K_SERO = 0.1
        DIM = 256
        key = jax.random.key(seed)
        ks = jax.random.split(key, 9)
        scale = 1.0 / np.sqrt(DIM)
        x = jax.random.normal(ks[0], (2, 512, DIM), dtype=jnp.float32)
        Wq = jax.random.normal(ks[1], (DIM, DIM), dtype=jnp.float32) * scale
        bq = jnp.zeros((DIM,), dtype=jnp.float32)
        Wk = jax.random.normal(ks[2], (DIM, DIM), dtype=jnp.float32) * scale
        bk = jnp.zeros((DIM,), dtype=jnp.float32)
        Wv = jax.random.normal(ks[3], (DIM, DIM), dtype=jnp.float32) * scale
        bv = jnp.zeros((DIM,), dtype=jnp.float32)
        Wo = jax.random.normal(ks[4], (DIM, DIM), dtype=jnp.float32) * scale
        bo = jnp.zeros((DIM,), dtype=jnp.float32)
        return {'x': x, 'Wq': Wq, 'bq': bq, 'Wk': Wk, 'bk': bk, 'Wv': Wv, 'bv': bv, 'Wo': Wo, 'bo': bo}
    _L0_attn_in = _L0_attn_setup()

    def _L0_ffn_setup():
        import jax, jax.numpy as jnp
        import numpy as np
        TOP_K = 2
        key = jax.random.key(seed)
        k1, k2, k3 = jax.random.split(key, 3)
        B, S, H, E = (4, 512, 256, 8)
        x = jax.random.normal(k1, (B, S, H), dtype=jnp.float32)
        gate_w = jax.random.normal(k2, (E, H), dtype=jnp.float32) / np.sqrt(H)
        gate_b = jnp.zeros((E,), dtype=jnp.float32)
        expert_w = jax.random.normal(k3, (E, H, H), dtype=jnp.float32) / np.sqrt(H)
        expert_b = jnp.zeros((E, H), dtype=jnp.float32)
        return {'x': x, 'gate_w': gate_w, 'gate_b': gate_b, 'expert_w': expert_w, 'expert_b': expert_b}
    _L0_ffn_in = _L0_ffn_setup()
    _d = {'L0_attn_x': _L0_attn_in['x'], 'L0_attn_Wq': _L0_attn_in['Wq'], 'L0_attn_bq': _L0_attn_in['bq'], 'L0_attn_Wk': _L0_attn_in['Wk'], 'L0_attn_bk': _L0_attn_in['bk'], 'L0_attn_Wv': _L0_attn_in['Wv'], 'L0_attn_bv': _L0_attn_in['bv'], 'L0_attn_Wo': _L0_attn_in['Wo'], 'L0_attn_bo': _L0_attn_in['bo'], 'L0_ffn_gate_w': _L0_ffn_in['gate_w'], 'L0_ffn_gate_b': _L0_ffn_in['gate_b'], 'L0_ffn_expert_w': _L0_ffn_in['expert_w'], 'L0_ffn_expert_b': _L0_ffn_in['expert_b']}
    _x0 = _d['L0_attn_x']
    _d['L0_attn_x'] = jax.random.normal(jax.random.fold_in(jax.random.key(seed), 1), (1, 4096, 256), dtype=_x0.dtype)
    del _x0
    return _d

def reference(L0_attn_x, L0_attn_Wq, L0_attn_bq, L0_attn_Wk, L0_attn_bk, L0_attn_Wv, L0_attn_bv, L0_attn_Wo, L0_attn_bo, L0_ffn_gate_w, L0_ffn_gate_b, L0_ffn_expert_w, L0_ffn_expert_b):

    def _L0_attn_ref(x, Wq, bq, Wk, bk, Wv, bv, Wo, bo):
        import jax, jax.numpy as jnp
        import numpy as np
        BASE_THETA = 0.5
        K_DOP = 0.2
        K_NOR = 0.15
        K_SERO = 0.1
        DIM = 256
        q = jnp.einsum('bsd,ed->bse', x, Wq) + bq
        k = jnp.einsum('bsd,ed->bse', x, Wk) + bk
        v = jnp.einsum('bsd,ed->bse', x, Wv) + bv
        qk = jnp.einsum('bsd,btd->bst', q, k)
        theta = BASE_THETA + K_DOP * jax.nn.sigmoid(qk) + K_NOR * jnp.tanh(qk) + K_SERO * jax.nn.relu(qk)
        attn = jax.nn.softmax(theta, axis=-1)
        out = jnp.einsum('bst,btd->bsd', attn, v)
        return jnp.einsum('bsd,ed->bse', out, Wo) + bo

    def _L0_ffn_ref(x, gate_w, gate_b, expert_w, expert_b):
        import jax, jax.numpy as jnp
        import numpy as np
        TOP_K = 2
        gates = jax.nn.softmax(jnp.einsum('bsh,eh->bse', x, gate_w) + gate_b, axis=-1)
        top_gates, top_idx = jax.lax.top_k(gates, TOP_K)
        expert_out = jnp.einsum('bsh,eoh->bseo', x, expert_w) + expert_b
        selected = jnp.take_along_axis(expert_out, top_idx[..., None], axis=2)
        return (selected * top_gates[..., None]).sum(axis=2)
    x = L0_attn_x
    xn = _layernorm(x, axis=-1)
    s = _L0_attn_ref(xn, L0_attn_Wq, L0_attn_bq, L0_attn_Wk, L0_attn_bk, L0_attn_Wv, L0_attn_bv, L0_attn_Wo, L0_attn_bo)
    g = _silu(_L0_ffn_ref(xn, L0_ffn_gate_w, L0_ffn_gate_b, L0_ffn_expert_w, L0_ffn_expert_b))
    x = x + s * g
    return x

_drawn_inputs = setup_inputs


def setup_inputs(seed=0):
    import zlib

    import numpy as np

    out = dict(_drawn_inputs(seed))
    spreads = {'L0_attn_bq': (0.0, 0.8),
     'L0_attn_bk': (0.0, 0.8),
     'L0_attn_bv': (0.0, 0.342),
     'L0_attn_bo': (0.0, 0.342),
     'L0_ffn_gate_b': (0.0, 0.8),
     'L0_ffn_expert_b': (0.0, 0.8)}
    factors = {}
    for name, (base, spread) in spreads.items():
        noise = np.random.default_rng([zlib.crc32(name.encode()), seed]).standard_normal(out[name].shape)
        drawn = base * np.exp(spread * noise) if base else spread * noise
        out[name] = jnp.asarray(drawn.astype(out[name].dtype))
    for name, factor in factors.items():
        out[name] = (out[name] * factor).astype(out[name].dtype)
    return out
```

```python
from contextlib import ExitStack

import concourse.bass as bass
from concourse import mybir

F32 = mybir.dt.float32
F32R = mybir.dt.float32r
I32 = mybir.dt.int32
ALU = mybir.AluOpType
ACT = mybir.ActivationFunctionType
AX = mybir.AxisListType

P = 128
S = 4096
D = 256
KD = D // P
E = 8
NT = S // P
GT = 2
NG = NT // GT
GW = GT * P
BANK = 512
NE = E * D // BANK
GC = E + 2
CH = 1024
CPT = S // CH
CPB = 2 * CPT
NB = NT // 2
HPC = CH // BANK
EXP_LAG = 5
T_LAG = 6
EPS = 1e-5
RSQRT_MAGIC = float(0x5F3759DF)


def after(engine, semaphore, count):
    if not isinstance(count, int) or count > 0:
        engine.wait_ge(semaphore, count)


def after_both(engine, semaphore, count, done, done_count):
    if not isinstance(count, int):
        count = engine.to_reg(count)
    engine.wait_ge(done, done_count)
    engine.wait_ge(semaphore, count)


def there(index, end):
    return not isinstance(index, int) or 0 <= index < end


class Steps:

    def __init__(self, engine, semaphore):
        self.engine, self.semaphore, self.base, self.n = engine, semaphore, 0, 0

    def wait_for(self, instruction):
        self.n += 1
        instruction.then_inc(self.semaphore, 1)
        self.engine.wait_ge(self.semaphore, self.base + self.n)


def passes(hi, lo, moving_hi, moving_lo):
    return ((hi, moving_hi), (hi, moving_lo), (lo, moving_hi))


def build(nc, x, wq, wk, wv, wo_t, cols, gate_t, gate_b, expert_t, expert_b, bo, out):
    g_dram = nc.dram_tensor("silu_gate_scratch", [S, D], F32).ap()
    x2, out2 = x[0], out[0]

    ctx = ExitStack()
    with ctx:
        def sb(name, shape, dt=F32, where=ctx):
            return where.enter_context(nc.sbuf_tensor(name, shape, dt))

        def ps(name, shape, where):
            return where.enter_context(nc.psum_tensor(name, shape, F32))

        def sem(name):
            return ctx.enter_context(nc.semaphore(name))

        xn_hi = sb("xn_hi", [P, KD, S], F32R)
        xn_lo = sb("xn_lo", [P, KD, S], F32R)
        vals = sb("vals", [P, NT, 2 * D], F32R)
        a_hi = sb("a_hi", [P, KD, D], F32R)
        a_lo = sb("a_lo", [P, KD, D], F32R)
        q_bias = sb("q_bias", [P, KD])
        o_bias = sb("o_bias", [P, D])
        r_all = sb("r_all", [P, NT])
        ident = sb("ident", [P, P])

        phase12 = ExitStack()
        b_hi = sb("b_hi", [P, KD, D], F32R, phase12)
        b_lo = sb("b_lo", [P, KD, D], F32R, phase12)
        gw_hi = sb("gw_hi", [P, KD, GC], F32R, phase12)
        gw_lo = sb("gw_lo", [P, KD, GC], F32R, phase12)
        ew_hi = sb("ew_hi", [P, KD, E * D], F32R, phase12)
        ew_lo = sb("ew_lo", [P, KD, E * D], F32R, phase12)
        eb = sb("eb", [E, D], F32, phase12)
        g_bias = sb("g_bias", [P, GT, GC], F32, phase12)
        desc = sb("desc", [P, GT, E], F32, phase12)

        with ExitStack() as ph:
            wq_sb = sb("wq_sb", [P, KD, D], F32, ph)
            wk_sb = sb("wk_sb", [P, KD, D], F32, ph)
            wv_sb = sb("wv_sb", [P, KD, D], F32, ph)
            wo_sb = sb("wo_sb", [P, KD, D], F32, ph)
            cols_sb = sb("cols_sb", [P, KD, 3], F32, ph)
            bq_wide = sb("bq_wide", [P, KD, P], F32, ph)
            bv_wide = sb("bv_wide", [P, KD, P], F32, ph)
            gb_sb = sb("gb_sb", [1, E], F32, ph)
            bo_sb = sb("bo_sb", [1, D], F32, ph)
            gw = sb("gw", [P, KD, GC], F32, ph)
            ew = sb("ew", [P, KD, E * D], F32, ph)
            ones = sb("ones", [1, P], F32, ph)
            desc_i = sb("desc_i", [P, GT, E], I32, ph)
            ps_a = ps("ps_a", [P, KD, D], ph)
            ps_b = ps("ps_b", [P, KD, D], ph)
            ps_o = ps("ps_o", [P, BANK], ph)
            ps_c = ps("ps_c", [P, BANK], ph)
            small_in, big_in = sem("small_in"), sem("big_in")
            pool_const, wide_done = sem("pool_const"), sem("wide_done")
            products, w_hi, w_steps = sem("products"), sem("w_hi"), sem("w_steps")
            SMALL = 9

            with nc.Block() as block:
                @block.sync
                def _(sp):
                    for tile, src in ((wq_sb, wq), (wk_sb, wk), (wv_sb, wv), (wo_sb, wo_t), (cols_sb, cols)):
                        sp.dma_start(tile[:], src.rearrange("(k p) n -> p k n", p=P)).then_inc(small_in, 16)
                    sp.dma_start(gw[:, :, 0:E], gate_t.rearrange("(k p) n -> p k n", p=P)).then_inc(small_in, 16)
                    sp.dma_start(gb_sb[:], gate_b).then_inc(small_in, 16)
                    sp.dma_start(bo_sb[:], bo).then_inc(small_in, 16)
                    sp.dma_start(eb[:], expert_b).then_inc(small_in, 16)

                @block.gpsimd
                def _(pool):
                    nc.gpsimd.memset(ident[:], 0.0).then_inc(pool_const, 1)
                    nc.gpsimd.memset(ones[:], 1.0).then_inc(pool_const, 1)
                    nc.gpsimd.iota(desc_i[:], [[0, GT], [-1, E]], base=E, channel_multiplier=0).then_inc(pool_const, 1)
                    pool.wait_ge(pool_const, 3)
                    nc.gpsimd.affine_select(out=ident[:], in_=ident[:], compare_op=ALU.not_equal, fill=1.0, base=0,
                                            pattern=[[-1, P]], channel_multiplier=1).then_inc(pool_const, 1)

                @block.tensor
                def _(pe):
                    pe.wait_ge(small_in, 16 * SMALL)
                    for acc, left, right in ((ps_a, wq_sb, wk_sb), (ps_b, wv_sb, wo_sb)):
                        for h in range(KD):
                            for k in range(KD):
                                mm = nc.tensor.matmul(acc[:, h, :], left[:, k, h * P:(h + 1) * P], right[:, k, :],
                                                      start=k == 0, stop=k == KD - 1)
                        mm.then_inc(products, 1)
                    for n, (left, col) in enumerate(((wk_sb, 0), (wq_sb, 1))):
                        for h in range(KD):
                            for k in range(KD):
                                nc.tensor.matmul(ps_c[:, n * KD + h:n * KD + h + 1], left[:, k, h * P:(h + 1) * P],
                                                 cols_sb[:, k, col:col + 1], start=k == 0, stop=k == KD - 1)
                    pe.wait_ge(pool_const, 4)
                    nc.tensor.matmul(ps_c[:, 8:8 + E], ones[:], gb_sb[:], start=True, stop=True)
                    pe.wait_ge(wide_done, 2)
                    for k in range(KD):
                        mm = nc.tensor.matmul(ps_c[:, 8 + E:9 + E], bq_wide[:, k, :], cols_sb[:, k, 1:2],
                                              start=k == 0, stop=k == KD - 1)
                    mm.then_inc(products, 1)
                    for k in range(KD):
                        nc.tensor.matmul(ps_o[:, 0:D], bv_wide[:, k, :], wo_sb[:, k, :], start=k == 0, stop=False)
                    nc.tensor.matmul(ps_o[:, 0:D], ones[:], bo_sb[:], start=False, stop=True).then_inc(products, 1)

                @block.scalar
                def _(act):
                    act.dma_start(ew[:], expert_t.rearrange("(k p) n -> p k n", p=P)).then_inc(big_in, 16)
                    act.wait_ge(products, 1)
                    nc.scalar.copy(a_hi[:], ps_a[:]).then_inc(w_hi, 1)
                    act.wait_ge(products, 2)
                    nc.scalar.copy(b_hi[:], ps_b[:]).then_inc(w_hi, 1)
                    act.wait_ge(big_in, 16)
                    for k in range(KD):
                        nc.scalar.copy(ew_hi[:, k, :], ew[:, k, :]).then_inc(w_hi, 1)

                @block.vector
                def _(dve):
                    nc.vector.memset(gw[:, :, E:GC], 0.0).then_inc(w_steps, 1)
                    nc.vector.memset(g_bias[:], 0.0).then_inc(w_steps, 1)
                    dve.wait_ge(pool_const, 3)
                    nc.vector.tensor_copy(desc[:], desc_i[:])
                    dve.wait_ge(small_in, 16 * SMALL)
                    nc.vector.tensor_copy(bq_wide[:], cols_sb[:, :, 0:1].broadcast_to([P, KD, P])).then_inc(wide_done, 1)
                    nc.vector.tensor_copy(bv_wide[:], cols_sb[:, :, 2:3].broadcast_to([P, KD, P])).then_inc(wide_done, 1)
                    dve.wait_ge(w_hi, 1)
                    nc.vector.tensor_tensor(a_lo[:], ps_a[:], a_hi[:].bitcast(F32), ALU.subtract)
                    dve.wait_ge(w_hi, 2)
                    nc.vector.tensor_tensor(b_lo[:], ps_b[:], b_hi[:].bitcast(F32), ALU.subtract)
                    dve.wait_ge(products, 3)
                    dve.wait_ge(w_steps, 2)
                    nc.vector.tensor_copy(q_bias[:], ps_c[:, 0:KD])
                    nc.vector.tensor_copy(gw[:, :, E], ps_c[:, KD:2 * KD]).then_inc(w_steps, 1)
                    for t in range(GT):
                        nc.vector.tensor_copy(g_bias[:, t, 0:E + 1], ps_c[:, 8:9 + E])
                    dve.wait_ge(w_steps, 3)
                    nc.vector.tensor_copy(gw_hi[:], gw[:]).then_inc(w_steps, 1)
                    dve.wait_ge(w_steps, 4)
                    nc.vector.tensor_tensor(gw_lo[:], gw[:], gw_hi[:].bitcast(F32), ALU.subtract)
                    dve.wait_ge(products, 4)
                    nc.vector.tensor_copy(o_bias[:], ps_o[:, 0:D])
                    for k in range(KD):
                        dve.wait_ge(w_hi, 3 + k)
                        nc.vector.tensor_tensor(ew_lo[:, k, :], ew[:, k, :], ew_hi[:, k, :].bitcast(F32), ALU.subtract)

        with ExitStack() as ph:
            x_in = sb("x_in", [P, 2, GT, D], F32, ph)
            xn = sb("xn", [P, GT, D], F32, ph)
            st_hi = sb("st_hi", [P, 2, KD, GW], F32R, ph)
            st_lo = sb("st_lo", [P, 2, KD, GW], F32R, ph)
            stats = sb("stats", [P, GT, 6], F32, ph)
            mv = sb("mv", [P, GT, 2], F32, ph)
            var = sb("var", [P, GT], F32, ph)
            rstd = sb("rstd", [P, GT], F32, ph)
            nwt = sb("nwt", [P, GT], F32, ph)
            logits = sb("logits", [P, GT, GC], F32, ph)
            lmax = sb("lmax", [P, GT, 1], F32, ph)
            ldiff = sb("ldiff", [P, GT, E], F32, ph)
            gexp = sb("gexp", [P, GT, E], F32, ph)
            gsum = sb("gsum", [P, GT, 1], F32, ph)
            ginv = sb("ginv", [P, GT, 1], F32, ph)
            cand = sb("cand", [P, GT, E], F32, ph)
            best = sb("best", [P, GT, 1], F32, ph)
            sel1 = sb("sel1", [P, GT, E], F32, ph)
            rest = sb("rest", [P, GT, E], F32, ph)
            sel2 = sb("sel2", [P, GT, E], F32, ph)
            wts = sb("wts", [P, 2, GT, E], F32, ph)
            wt_t = sb("wt_t", [E, GW], F32, ph)
            acc = sb("acc", [P, 2, GT, D], F32, ph)
            tnh = sb("tnh", [P, GT, D], F32, ph)
            g_sb = sb("g_sb", [P, 2, GT, D], F32, ph)
            ps_x = ps("ps_x", [P, KD, GW], ph)
            ps_v = ps("ps_v", [P, GT, D], ph)
            ps_g = ps("ps_g", [P, BANK], ph)
            ps_y = ps("ps_y", [P, GT, D], ph)
            ps_e = [ps(f"ps_e{n}", [P, BANK], ph) for n in range(NE)]
            ps_wt = ps_g[0:E, P:P + GW]

            x_loaded = [sem("x_loaded0"), sem("x_loaded1")]
            g_stored = sem("g_stored")
            xn_ready, xt_ready, xt_hi, xt_lo, kept = map(sem, ("xn_ready", "xt_ready", "xt_hi", "xt_lo", "kept"))
            logits_ready, ldiff_ready, gexp_ready = map(sem, ("logits_ready", "ldiff_ready", "gexp_ready"))
            w_ready, wt_ready, wt_sb_ready = map(sem, ("w_ready", "wt_ready", "wt_sb_ready"))
            yb_ready, acc_ready, v_ready, v_hi, v_lo = map(sem, ("yb_ready", "acc_ready", "v_ready", "v_hi", "v_lo"))
            ex_ready, ex_used, tnh_ready, g_ready = map(sem, ("ex_ready", "ex_used", "tnh_ready", "g_ready"))
            v_steps = sem("v_steps")

            def bodies(engine, body):
                body(0)
                with engine.Fori(1, NG // 2 - 1) as j:
                    body(j)
                body(NG // 2 - 1)

            with nc.Block() as block:
                @block.sync
                def _(sp):
                    def load(f, par, uses):
                        after(sp, xn_ready, f - 1)
                        sp.dma_start(x_in[:, par], x2[bass.ds(f * GW, GW), :].rearrange("(t p) d -> p t d", p=P)
                                     ).then_inc(x_loaded[par], 16)

                    def store(u, par):
                        sp.wait_ge(g_ready, u + 1)
                        sp.dma_start(g_dram[bass.ds(u * GW, GW), :].rearrange("(t p) d -> p t d", p=P),
                                     g_sb[:, par]).then_inc(g_stored, 16)

                    def body(j):
                        for p in range(2):
                            u = 2 * j + p
                            if there(u + 2, NG):
                                load(u + 2, p, j + 1)
                            if there(u - 1, NG):
                                store(u - 1, 1 - p)

                    load(0, 0, 0)
                    load(1, 1, 0)
                    bodies(sp, body)
                    store(NG - 1, (NG - 1) % 2)
                    sp.wait_ge(g_stored, 16 * NG)

                @block.gpsimd
                def _(pool):
                    def keep(f, par):
                        after_both(pool, xt_lo, f + 1, pool_const, 4)
                        nc.gpsimd.tensor_copy(xn_hi[:, :, bass.ds(f * GW, GW)], st_hi[:, par].bitcast(F32))
                        nc.gpsimd.tensor_copy(xn_lo[:, :, bass.ds(f * GW, GW)], st_lo[:, par].bitcast(F32)
                                              ).then_inc(kept, 1)

                    def body(j):
                        for p in range(2):
                            if there(2 * j + p + 1, NG):
                                keep(2 * j + p + 1, 1 - p)

                    keep(0, 0)
                    bodies(pool, body)

                @block.tensor
                def _(pe):
                    def transposes(f):
                        pe.wait_ge(xn_ready, f + 1)
                        after(pe, xt_lo, f)
                        for t in range(GT):
                            for k in range(KD):
                                tr = nc.tensor.transpose(ps_x[:, k, t * P:(t + 1) * P], xn[:, t, k * P:(k + 1) * P],
                                                         ident[:])
                        tr.then_inc(xt_ready, 1)

                    def project(acc_of, w_pair, par):
                        for t in range(GT):
                            n = 0
                            for k in range(KD):
                                hi, lo = (s[:, par, k, t * P:(t + 1) * P] for s in (st_hi, st_lo))
                                for left, right in passes(hi, lo, w_pair[0][:, k, :], w_pair[1][:, k, :]):
                                    mm = nc.tensor.matmul(acc_of(t), left, right, start=n == 0, stop=n == 3 * KD - 1)
                                    n += 1
                        return mm

                    def gates(f, par):
                        pe.wait_ge(xt_lo, f + 1)
                        after(pe, wt_sb_ready, f)
                        project(lambda t: ps_g[:, t * GC:(t + 1) * GC], (gw_hi, gw_lo), par).then_inc(logits_ready, 1)

                    def values(f, par):
                        after(pe, v_lo, f)
                        project(lambda t: ps_v[:, t, :], (b_hi, b_lo), par).then_inc(v_ready, 1)

                    def weights_t(f, par):
                        pe.wait_ge(w_ready, f + 1)
                        for t in range(GT):
                            tr = nc.tensor.transpose(ps_wt[:, t * P:(t + 1) * P], wts[:, par, t, :], ident[:])
                        tr.then_inc(wt_ready, 1)

                    def bias_mix(f):
                        pe.wait_ge(wt_sb_ready, f + 1)
                        after(pe, acc_ready, f)
                        for t in range(GT):
                            mm = nc.tensor.matmul(ps_y[:, t, :], wt_t[:, t * P:(t + 1) * P], eb[:], start=True, stop=True)
                        mm.then_inc(yb_ready, 1)

                    def expert(u, par, t, b):
                        after(pe, ex_used, u * 2 * NE + t * NE + b - NE + 1)
                        n = 0
                        for k in range(KD):
                            hi, lo = (s[:, par, k, t * P:(t + 1) * P] for s in (st_hi, st_lo))
                            for left, right in passes(hi, lo, *(w[:, k, b * BANK:(b + 1) * BANK] for w in (ew_hi, ew_lo))):
                                mm = nc.tensor.matmul(ps_e[b][:], left, right, start=n == 0, stop=n == 3 * KD - 1)
                                n += 1
                        mm.then_inc(ex_ready, 1)

                    def body(j):
                        for p in range(2):
                            u, f = 2 * j + p, 2 * j + p + 1
                            more = there(f, NG)
                            expert(u, p, 0, 0)
                            expert(u, p, 0, 1)
                            if more:
                                transposes(f)
                            expert(u, p, 0, 2)
                            expert(u, p, 0, 3)
                            if more:
                                gates(f, 1 - p)
                                values(f, 1 - p)
                            expert(u, p, 1, 0)
                            expert(u, p, 1, 1)
                            if more:
                                weights_t(f, 1 - p)
                            expert(u, p, 1, 2)
                            if more:
                                bias_mix(f)
                            expert(u, p, 1, 3)

                    transposes(0)
                    gates(0, 0)
                    values(0, 0)
                    weights_t(0, 0)
                    bias_mix(0)
                    bodies(pe, body)

                @block.scalar
                def _(act):
                    def split_xt(f, par):
                        act.wait_ge(xt_ready, f + 1)
                        after(act, ex_ready, 2 * NE * f - 2 * NE)
                        after(act, kept, f - 1)
                        nc.scalar.copy(st_hi[:, par], ps_x[:]).then_inc(xt_hi, 1)

                    def gate_exp(f):
                        act.wait_ge(ldiff_ready, f + 1)
                        nc.scalar.activation(gexp[:], ldiff[:], ACT.Exp).then_inc(gexp_ready, 1)

                    def split_v(f):
                        after_both(act, v_ready, f + 1, w_hi, 4)
                        nc.scalar.copy(vals[:, bass.ds(f * GT, GT), 0:D], ps_v[:]).then_inc(v_hi, 1)

                    def weights_t(f):
                        act.wait_ge(wt_ready, f + 1)
                        after(act, yb_ready, f)
                        nc.scalar.copy(wt_t[:], ps_wt).then_inc(wt_sb_ready, 1)

                    def start_acc(f, par):
                        act.wait_ge(yb_ready, f + 1)
                        after(act, g_ready, f - 1)
                        nc.scalar.copy(acc[:, par], ps_y[:]).then_inc(acc_ready, 1)

                    def tanh_acc(u, par):
                        act.wait_ge(ex_used, u * 2 * NE + 2 * NE)
                        after(act, g_ready, u)
                        nc.scalar.activation(tnh[:], acc[:, par], ACT.Tanh).then_inc(tnh_ready, 1)

                    def front(f, par):
                        split_xt(f, par)
                        gate_exp(f)
                        split_v(f)
                        weights_t(f)
                        start_acc(f, par)

                    def body(j):
                        for p in range(2):
                            if there(2 * j + p + 1, NG):
                                front(2 * j + p + 1, 1 - p)
                            tanh_acc(2 * j + p, p)

                    front(0, 0)
                    bodies(act, body)

                @block.vector
                def _(dve):
                    step = Steps(dve, v_steps)

                    def split_xt(f, par):
                        dve.wait_ge(xt_hi, f + 1)
                        nc.vector.tensor_tensor(st_lo[:, par], ps_x[:], st_hi[:, par].bitcast(F32), ALU.subtract
                                                ).then_inc(xt_lo, 1)

                    def split_v(f):
                        dve.wait_ge(v_hi, f + 1)
                        nc.vector.tensor_tensor(vals[:, bass.ds(f * GT, GT), D:2 * D], ps_v[:],
                                                vals[:, bass.ds(f * GT, GT), 0:D].bitcast(F32), ALU.subtract
                                                ).then_inc(v_lo, 1)

                    def top2(f, par):
                        wide = [P, GT, E]
                        dve.wait_ge(logits_ready, f + 1)
                        step.wait_for(nc.vector.tensor_tensor(
                            logits[:], ps_g[:, 0:GT * GC].rearrange("p (t c) -> p t c", c=GC), g_bias[:], ALU.add))
                        nc.vector.tensor_scalar(r_all[:, bass.ds(f * GT, GT)], logits[:, :, E], 1.0, None, ALU.mult)
                        step.wait_for(nc.vector.tensor_reduce(lmax[:], logits[:, :, 0:E], AX.X, ALU.max))
                        nc.vector.tensor_tensor(ldiff[:], logits[:, :, 0:E], lmax[:].broadcast_to(wide), ALU.subtract
                                                ).then_inc(ldiff_ready, 1)
                        dve.wait_ge(gexp_ready, f + 1)
                        nc.vector.tensor_reduce(gsum[:], gexp[:], AX.X, ALU.add).then_inc(v_steps, 1)
                        step.n += 1
                        step.wait_for(nc.vector.scalar_tensor_tensor(cand[:], gexp[:], 1.0, desc[:], ALU.is_ge, ALU.mult))
                        nc.vector.reciprocal(ginv[:], gsum[:])
                        step.wait_for(nc.vector.tensor_reduce(best[:], cand[:], AX.X, ALU.max))
                        step.wait_for(nc.vector.tensor_tensor(sel1[:], desc[:], best[:].broadcast_to(wide), ALU.is_equal))
                        step.wait_for(nc.vector.scalar_tensor_tensor(rest[:], sel1[:], -2.0, gexp[:], ALU.mult, ALU.add))
                        step.wait_for(nc.vector.tensor_reduce(best[:], rest[:], AX.X, ALU.max))
                        step.wait_for(nc.vector.tensor_tensor(cand[:], rest[:], best[:].broadcast_to(wide), ALU.is_equal))
                        step.wait_for(nc.vector.tensor_tensor(cand[:], cand[:], desc[:], ALU.mult))
                        step.wait_for(nc.vector.tensor_reduce(best[:], cand[:], AX.X, ALU.max))
                        step.wait_for(nc.vector.tensor_tensor(sel2[:], desc[:], best[:].broadcast_to(wide), ALU.is_equal))
                        step.wait_for(nc.vector.tensor_tensor(sel2[:], sel1[:], sel2[:], ALU.add))
                        step.wait_for(nc.vector.tensor_tensor(sel2[:], sel2[:], gexp[:], ALU.mult))
                        nc.vector.scalar_tensor_tensor(wts[:, par], sel2[:], 0.5, ginv[:].broadcast_to(wide),
                                                       ALU.mult, ALU.mult).then_inc(w_ready, 1)

                    def combine(u, par, t, b):
                        if t == 0 and b == 0:
                            dve.wait_ge(acc_ready, u + 1)
                            dve.wait_ge(w_ready, u + 1)
                        dve.wait_ge(ex_ready, u * 2 * NE + t * NE + b + 1)
                        a = acc[:, par, t, :]
                        step.wait_for(nc.vector.scalar_tensor_tensor(
                            a, ps_e[b][:, 0:D], wts[:, par, t, 2 * b:2 * b + 1], a, ALU.mult, ALU.add))
                        nc.vector.scalar_tensor_tensor(
                            a, ps_e[b][:, D:2 * D], wts[:, par, t, 2 * b + 1:2 * b + 2], a, ALU.mult, ALU.add
                            ).then_inc(ex_used, 1)
                        dve.wait_ge(ex_used, u * 2 * NE + t * NE + b + 1)

                    def silu(u, par):
                        dve.wait_ge(tnh_ready, u + 1)
                        after(dve, g_stored, 16 * u)
                        nc.vector.scalar_tensor_tensor(g_sb[:, par], tnh[:], 1.0, acc[:, par], ALU.add, ALU.mult
                                                       ).then_inc(g_ready, 1)

                    def layer_norm(f, par, uses):
                        dve.wait_ge(x_loaded[par], 16 * uses)
                        nc.vector.bn_stats(stats[:, 0, :], x_in[:, par, 0, :])
                        nc.vector.bn_stats(stats[:, 1, :], x_in[:, par, 1, :]).then_inc(v_steps, 1)
                        step.n += 1
                        after_both(dve, v_steps, step.base + step.n, w_steps, 4)
                        nc.vector.bn_aggr(mv[:, 0, :], stats[:, 0, :])
                        step.wait_for(nc.vector.bn_aggr(mv[:, 1, :], stats[:, 1, :]))
                        step.wait_for(nc.vector.tensor_scalar(var[:], mv[:, :, 1], EPS, None, ALU.add))
                        step.wait_for(nc.vector.tensor_scalar(rstd[:].bitcast(I32), var[:].bitcast(I32), -0.5,
                                                              RSQRT_MAGIC, ALU.mult, ALU.add))
                        for _ in range(3):
                            step.wait_for(nc.vector.tensor_tensor(nwt[:], rstd[:], rstd[:], ALU.mult))
                            step.wait_for(nc.vector.tensor_tensor(nwt[:], nwt[:], var[:], ALU.mult))
                            step.wait_for(nc.vector.tensor_scalar(nwt[:], nwt[:], -0.5, 1.5, ALU.mult, ALU.add))
                            step.wait_for(nc.vector.tensor_tensor(rstd[:], rstd[:], nwt[:], ALU.mult))
                        after(dve, xt_ready, f)
                        for t in range(GT):
                            last = nc.vector.tensor_scalar(xn[:, t, :], x_in[:, par, t, :], mv[:, t, 0:1],
                                                           rstd[:, t:t + 1], ALU.subtract, ALU.mult)
                        last.then_inc(xn_ready, 1)

                    def body(j):
                        for p in range(2):
                            u, f = 2 * j + p, 2 * j + p + 1
                            more = there(f, NG)
                            combine(u, p, 0, 0)
                            if there(u - 1, NG):
                                silu(u - 1, 1 - p)
                            combine(u, p, 0, 1)
                            if more:
                                split_xt(f, 1 - p)
                            combine(u, p, 0, 2)
                            combine(u, p, 0, 3)
                            if more:
                                top2(f, 1 - p)
                                split_v(f)
                            for b in range(NE):
                                combine(u, p, 1, b)
                            if there(u + 2, NG):
                                layer_norm(u + 2, p, j + 2)

                    layer_norm(0, 0, 1)
                    split_xt(0, 0)
                    layer_norm(1, 1, 1)
                    top2(0, 0)
                    split_v(0)
                    ahead = step.n
                    body(0)
                    per_body = step.n - ahead
                    with dve.Fori(1, NG // 2 - 1) as j:
                        step.base, step.n = j * per_body, ahead
                        body(j)
                        assert step.n == ahead + per_body
                    step.base, step.n = 0, ahead + per_body * (NG // 2 - 1)
                    body(NG // 2 - 1)
                    silu(NG - 1, (NG - 1) % 2)
        phase12.close()

        with ExitStack() as ph:
            th = sb("th", [P, 2, CH], F32, ph)
            tz = sb("tz", [P, 2, CH], F32, ph)
            ring = sb("ring", [P, CPB, CH], F32, ph)
            p_hi = sb("p_hi", [P, 2, BANK], F32R, ph)
            p_lo = sb("p_lo", [P, 2, BANK], F32R, ph)
            q_hi = sb("q_hi", [P, KD, GW], F32R, ph)
            q_lo = sb("q_lo", [P, KD, GW], F32R, ph)
            r_cur = sb("r_cur", [P, 2, 3], F32, ph)
            cmax = sb("cmax", [P, 2, CPT], F32, ph)
            nmax = sb("nmax", [P, 2], F32, ph)
            e_bias = sb("e_bias", [P, 2], F32, ph)
            csum = sb("csum", [P, 2, CPT], F32, ph)
            rsum = sb("rsum", [P, 2], F32, ph)
            rinv = sb("rinv", [P, 2], F32, ph)
            o_lo = sb("o_lo", [P, D], F32, ph)
            att = sb("att", [P, 2, D], F32, ph)
            x_in3 = sb("x_in3", [P, 2, D], F32, ph)
            g_in3 = sb("g_in3", [P, 2, D], F32, ph)
            y_out = sb("y_out", [P, 2, D], F32, ph)
            ps_s = ps("ps_s", [P, 2, CH], ph)
            ps_t = ps("ps_t", [P, 2, BANK], ph)
            ps_o3 = ps("ps_o3", [P, 2, 2 * D], ph)

            xg_loaded = [sem("xg_loaded0"), sem("xg_loaded1")]
            y_stored = [sem("y_stored0"), sem("y_stored1")]
            scores, tanh_done, a_done, b_done, max_done = map(sem, ("scores", "tanh_done", "a_done", "b_done", "max_done"))
            nmax_done, bias_ready, exp_done, r_ready = map(sem, ("nmax_done", "bias_ready", "exp_done", "r_ready"))
            t_ready, hi_done, lo_done, pv_done = map(sem, ("t_ready", "hi_done", "lo_done", "pv_done"))
            rsum_done, rinv_ready, o_lo_ready, out_read = map(sem, ("rsum_done", "rinv_ready", "o_lo_ready", "out_read"))
            fin_steps, y_ready = sem("fin_steps"), sem("y_ready")

            PER_BODY = 2 * CPB + KD

            def t_use(j, c, half):
                q_uses = 2 if not isinstance(j, int) or j < NB else 2 - KD
                before = 0
                if c < 0:
                    c, before = c + CPB, PER_BODY
                return j * PER_BODY + (2 * (c - T_LAG) + half + q_uses - before)

            def q_use(j, half):
                if isinstance(j, int) and j == 0:
                    return half
                return j * PER_BODY + (t_use(-1, CPB - 1, 1) + 1 + half)

            def bodies3(engine, body):
                body(0)
                body(1)
                with engine.Fori(2, NB - 1) as j:
                    body(j)
                body(NB - 1)
                body(NB)

            with nc.Block() as block:
                @block.sync
                def _(sp):
                    def load(i, par):
                        after(sp, y_ready, i - 1)
                        rows = bass.ds(i * P, P)
                        sp.dma_start(x_in3[:, par], x2[rows, :]).then_inc(xg_loaded[par], 16)
                        sp.dma_start(g_in3[:, par], g_dram[rows, :]).then_inc(xg_loaded[par], 16)

                    def body(j):
                        for p in range(2):
                            if there(2 * j - 2 + p, NT):
                                sp.wait_ge(y_ready, 2 * j - 1 + p)
                                sp.dma_start(out2[bass.ds((2 * j - 2 + p) * P, P), :], y_out[:, p]
                                             ).then_inc(y_stored[p], 16)
                            if there(2 * j + p, NT):
                                load(2 * j + p, p)

                    bodies3(sp, body)
                    for p in range(2):
                        sp.wait_ge(y_stored[p], 16 * NT // 2)

                @block.tensor
                def _(pe):
                    def queries(j):
                        for half in range(KD):
                            n, bank = q_use(j, half), half
                            after(pe, lo_done, n - 1)
                            i = 0
                            for k in range(KD):
                                hi, lo = (a[:, k, half * P:(half + 1) * P] for a in (a_hi, a_lo))
                                toks = bass.ds(j * GW, GW)
                                for left, right in passes(hi, lo, xn_hi[:, k, toks], xn_lo[:, k, toks]):
                                    mm = nc.tensor.matmul(ps_t[:, bank, 0:GW], left, right, start=i == 0,
                                                          stop=i == 3 * KD - 1)
                                    i += 1
                            mm.then_inc(t_ready, 1)

                    def score(c, bank):
                        i = 0
                        keys = slice((c % CPT) * CH + bank * BANK, (c % CPT) * CH + (bank + 1) * BANK)
                        row = slice(c // CPT * P, (c // CPT + 1) * P)
                        for k in range(KD):
                            for left, right in passes(q_hi[:, k, row], q_lo[:, k, row], xn_hi[:, k, keys], xn_lo[:, k, keys]):
                                mm = nc.tensor.matmul(ps_s[:, c % 2, bank * BANK:(bank + 1) * BANK], left, right,
                                                      start=i == 0, stop=i == 3 * KD - 1)
                                i += 1
                        return mm

                    def transposes(j, c, half):
                        n = t_use(j, c, half)
                        after(pe, lo_done, n - 1)
                        for b in range(BANK // P):
                            key = half * BANK + b * P
                            tr = nc.tensor.transpose(ps_t[:, half, b * P:(b + 1) * P],
                                                     ring[:, (c - T_LAG) % CPB, key:key + P], ident[:])
                        tr.then_inc(t_ready, 1)

                    def weigh(j, c, half):
                        h = (c - T_LAG) % CPB
                        first = h % CPT == 0 and half == 0
                        if first:
                            tile = 2 * j + (c - T_LAG) // CPT
                            after(pe, out_read, tile - 1)
                        pe.wait_ge(lo_done, t_use(j, c, half) + 1)
                        o = ps_o3[:, h // CPT]
                        for b in range(BANK // P):
                            key_tile = (h % CPT) * (CH // P) + half * (BANK // P) + b
                            hi, lo = (p[:, half, b * P:(b + 1) * P] for p in (p_hi, p_lo))
                            end = h % CPT == CPT - 1 and half == 1 and b == BANK // P - 1
                            nc.tensor.matmul(o[:], hi, vals[:, key_tile, :], start=first and b == 0, stop=False,
                                             skip_group_check=True)
                            mm = nc.tensor.matmul(o[:, 0:D], lo, vals[:, key_tile, 0:D], start=False, stop=end,
                                                  skip_group_check=True)
                        mm.then_inc(pv_done, 1)

                    def body(j):
                        for c in range(CPB):
                            s = CPB * j + c
                            make, use, used = there(s, NB * CPB), there(s - T_LAG, NB * CPB), there(s - T_LAG - 1, NB * CPB)
                            if make and c == 0:
                                q_wait = q_use(j, 1) + 1
                            if make and c > 0:
                                after(pe, a_done, s - 1)
                                score(c, 0)
                            if use:
                                pe.wait_ge(exp_done, s - T_LAG + 1)
                                transposes(j, c, 0)
                                transposes(j, c, 1)
                            if used:
                                weigh(j - 1 if c == 0 else j, (c - 1) % CPB, 1)
                            if make:
                                if c == 0:
                                    pe.wait_ge(lo_done, q_wait)
                                    after(pe, a_done, s - 1)
                                    score(c, 0)
                                score(c, 1).then_inc(scores, 1)
                            if c == CPB - 1 and there(j + 1, NB):
                                queries(j + 1)
                            if use:
                                weigh(j, c, 0)

                    queries(0)
                    bodies3(pe, body)

                @block.scalar
                def _(act):
                    def split_p(j, c, half):
                        n = t_use(j, c, half)
                        act.wait_ge(t_ready, n + 1)
                        after(act, pv_done, 2 * CPB * j + 2 * (c - T_LAG) + half - 1)
                        nc.scalar.copy(p_hi[:, half], ps_t[:, half]).then_inc(hi_done, 1)

                    def split_q(j):
                        for half in range(KD):
                            act.wait_ge(t_ready, q_use(j, half) + 1)
                            nc.scalar.activation(q_hi[:, half, :], ps_t[:, half, 0:GW], ACT.Identity,
                                                 bias=q_bias[:, half:half + 1]).then_inc(hi_done, 1)

                    def body(j):
                        for c in range(CPB):
                            s = CPB * j + c
                            if there(s - EXP_LAG, NB * CPB):
                                e = (c - EXP_LAG) % CPB
                                tile = 2 * j + (c - EXP_LAG) // CPT
                                if e % CPT == 0:
                                    act.wait_ge(bias_ready, tile + 1)
                                    after(act, rinv_ready, tile - 1)
                                nc.scalar.activation(ring[:, e], ring[:, e], ACT.Exp, scale=0.1,
                                                     bias=e_bias[:, e // CPT:e // CPT + 1],
                                                     accum_out=csum[:, e // CPT, e % CPT:e % CPT + 1]
                                                     ).then_inc(exp_done, 1)
                            if there(s - T_LAG, NB * CPB):
                                split_p(j, c, 0)
                                split_p(j, c, 1)
                            if c % CPT == 2 and there(s - 2 * CPT - 2, NB * CPB):
                                i, par = 2 * j + c // CPT - 2, c // CPT
                                act.wait_ge(pv_done, i * 2 * CPT + 2 * CPT)
                                act.wait_ge(rinv_ready, i + 1)
                                after(act, out_read, i)
                                nc.scalar.activation(o_lo[:], ps_o3[:, par, D:2 * D], ACT.Copy,
                                                     scale=rinv[:, par:par + 1]).then_inc(o_lo_ready, 1)
                            if c == CPB - 1 and there(j + 1, NB):
                                split_q(j + 1)
                            if there(s, NB * CPB):
                                act.wait_ge(scores, s + 1)
                                after(act, b_done, s - 1)
                                if c % CPT == 0:
                                    act.wait_ge(r_ready, 2 * j + c // CPT + 1)
                                nc.scalar.activation(th[:, c % 2], ps_s[:, c % 2], ACT.Tanh, scale=0.5,
                                                     bias=r_cur[:, c // CPT, 1:2])
                                nc.scalar.activation(tz[:, c % 2], ps_s[:, c % 2], ACT.Tanh,
                                                     bias=r_cur[:, c // CPT, 0:1]).then_inc(tanh_done, 1)

                    split_q(0)
                    bodies3(act, body)

                @block.vector
                def _(dve):
                    def row_terms(tile, par):
                        src = r_all[:, bass.ds(tile, 1)]
                        for n, factor in enumerate((1.0, 0.5, -1.0)):
                            last = nc.vector.tensor_scalar(r_cur[:, par, n:n + 1], src, factor, None, ALU.mult)
                        last.then_inc(r_ready, 1)

                    def split_p(j, c, half):
                        dve.wait_ge(hi_done, t_use(j, c, half) + 1)
                        nc.vector.tensor_tensor(p_lo[:, half], ps_t[:, half], p_hi[:, half].bitcast(F32), ALU.subtract
                                                ).then_inc(lo_done, 1)

                    def split_q(j):
                        for half in range(KD):
                            dve.wait_ge(hi_done, q_use(j, half) + 1)
                            nc.vector.scalar_tensor_tensor(q_lo[:, half, :], ps_t[:, half, 0:GW],
                                                           q_bias[:, half:half + 1], q_hi[:, half, :].bitcast(F32),
                                                           ALU.add, ALU.subtract).then_inc(lo_done, 1)

                    def body(j):
                        for c in range(CPB):
                            s = CPB * j + c
                            k = (c - 1) % CPB
                            tile, par = 2 * j + (c - 1) // CPT, k // CPT
                            score_there, p_there = there(s - 1, NB * CPB), there(s - T_LAG, NB * CPB)
                            if score_there:
                                dve.wait_ge(tanh_done, s)
                                nc.vector.scalar_tensor_tensor(th[:, k % 2], ps_s[:, k % 2], r_cur[:, par, 2:3],
                                                               th[:, k % 2], ALU.max, ALU.add).then_inc(a_done, 1)
                            if p_there:
                                split_p(j, c, 0)
                            if score_there:
                                dve.wait_ge(a_done, s)
                                if there(s - 1 - CPB, NB * CPB):
                                    dve.wait_ge(t_ready, t_use(j, c - 1 - CPB + T_LAG, 1) + 1)
                                nc.vector.scalar_tensor_tensor(ring[:, k], tz[:, k % 2], 1.5, th[:, k % 2],
                                                               ALU.mult, ALU.add).then_inc(b_done, 1)
                            if p_there:
                                split_p(j, c, 1)
                            if score_there:
                                dve.wait_ge(b_done, s)
                                nc.vector.tensor_reduce(cmax[:, par, k % CPT:k % CPT + 1], ring[:, k], AX.X, ALU.max
                                                        ).then_inc(max_done, 1)
                                if k % CPT == CPT - 1:
                                    dve.wait_ge(max_done, s)
                                    nc.vector.tensor_reduce(nmax[:, par:par + 1], cmax[:, par], AX.X, ALU.max,
                                                            negate=True).then_inc(nmax_done, 1)
                                    dve.wait_ge(nmax_done, tile + 1)
                                    after(dve, exp_done, CPT * (tile - 1))
                                    nc.vector.tensor_scalar(e_bias[:, par:par + 1], nmax[:, par:par + 1], 0.1, None,
                                                            ALU.mult).then_inc(bias_ready, 1)
                            if c % CPT == 1 and there(s - 2 * CPT - 1, NB * CPB):
                                i, q = 2 * j + c // CPT - 2, c // CPT
                                dve.wait_ge(exp_done, CPT * i + CPT)
                                nc.vector.tensor_reduce(rsum[:, q:q + 1], csum[:, q], AX.X, ALU.add).then_inc(rsum_done, 1)
                                dve.wait_ge(rsum_done, i + 1)
                                nc.vector.reciprocal(rinv[:, q:q + 1], rsum[:, q:q + 1]).then_inc(rinv_ready, 1)
                            if c % CPT == 2 and there(s - 2 * CPT - 2, NB * CPB):
                                i, q = 2 * j + c // CPT - 2, c // CPT
                                dve.wait_ge(o_lo_ready, i + 1)
                                after(dve, y_ready, i - 1)
                                nc.vector.scalar_tensor_tensor(att[:, q], ps_o3[:, q, 0:D], rinv[:, q:q + 1], o_lo[:],
                                                               ALU.mult, ALU.add).then_inc(out_read, 1)
                            if c == 1 and there(j, NB):
                                row_terms(2 * j + 1, 1)
                            if c == CPB - 2 and there(j + 1, NB):
                                row_terms(2 * j + 2, 0)
                            if c == CPB - 1 and there(j + 1, NB):
                                split_q(j + 1)

                    row_terms(0, 0)
                    split_q(0)
                    bodies3(dve, body)

                @block.gpsimd
                def _(pool):
                    def finish(i, par, uses):
                        a = att[:, par]
                        pool.wait_ge(out_read, i + 1)
                        nc.gpsimd.tensor_tensor(a, a, o_bias[:], ALU.add).then_inc(fin_steps, 1)
                        pool.wait_ge(fin_steps, 2 * i + 1)
                        pool.wait_ge(xg_loaded[par], 32 * uses)
                        nc.gpsimd.tensor_tensor(a, a, g_in3[:, par], ALU.mult).then_inc(fin_steps, 1)
                        pool.wait_ge(fin_steps, 2 * i + 2)
                        after(pool, y_stored[par], 16 * (uses - 1))
                        nc.gpsimd.tensor_tensor(y_out[:, par], a, x_in3[:, par], ALU.add).then_inc(y_ready, 1)

                    def body(j):
                        for p in range(2):
                            if there(2 * j - 2 + p, NT):
                                finish(2 * j - 2 + p, p, j)

                    bodies3(pool, body)


def kernel(**inputs):
    import numpy as np
    import concourse.bacc as bacc
    from concourse.bass_utils import run_bass_kernel_spmd

    def given(name):
        return np.asarray(inputs[name])

    arrays = {
        "x": given("L0_attn_x"),
        "wq": given("L0_attn_Wq"),
        "wk": given("L0_attn_Wk"),
        "wv": given("L0_attn_Wv"),
        "wo_t": given("L0_attn_Wo").T,
        "cols": np.stack([given("L0_attn_bq"), given("L0_attn_bk"), given("L0_attn_bv")], axis=1),
        "gate_t": given("L0_ffn_gate_w").T,
        "gate_b": given("L0_ffn_gate_b")[None, :],
        "expert_t": given("L0_ffn_expert_w").reshape(E * D, D).T,
        "expert_b": given("L0_ffn_expert_b"),
        "bo": given("L0_attn_bo")[None, :],
    }
    nc = bacc.Bacc("TRN2", target_bir_lowering=False, num_devices=1)
    feeds, args = {}, []
    for name, a in arrays.items():
        a = np.ascontiguousarray(a)
        feeds[f"in_{name}"] = a
        args.append(nc.dram_tensor(f"in_{name}", a.shape, mybir.dt.from_np(a.dtype), kind="ExternalInput").ap())
    out = nc.dram_tensor("out_y", [1, S, D], F32, kind="ExternalOutput").ap()
    build(nc, *args, out)
    result = run_bass_kernel_spmd(nc, [feeds], core_ids=[0])
    return result.results[0]["out_y"]
```

```python
from contextlib import ExitStack

import concourse.bass as bass
from concourse import mybir

F32 = mybir.dt.float32
F32R = mybir.dt.float32r
I32 = mybir.dt.int32
U32 = mybir.dt.uint32
ALU = mybir.AluOpType
ACT = mybir.ActivationFunctionType
AX = mybir.AxisListType

P = 128
S = 4096
D = 256
KD = D // P
E = 8
NT = S // P
GT = 2
NG = NT // GT
GW = GT * P
BANK = 512
ROW_STEP = 32
ROWS = 3 * ROW_STEP
NE = E * D // BANK
GC = E + 2
CH = 1024
CPT = S // CH
CPB = 2 * CPT
NB = NT // 2
EXP_LAG = 5
T_LAG = 6
EPS = 1e-5
RSQRT_MAGIC = float(0x5F3759DF)


def after(engine, semaphore, count):
    if not isinstance(count, int) or count > 0:
        engine.wait_ge(semaphore, count)


def after_both(engine, semaphore, count, done, done_count):
    if not isinstance(count, int):
        count = engine.to_reg(count)
    engine.wait_ge(done, done_count)
    engine.wait_ge(semaphore, count)


def there(index, end):
    return not isinstance(index, int) or 0 <= index < end


class Steps:

    def __init__(self, engine, semaphore):
        self.engine, self.semaphore, self.base, self.n = engine, semaphore, 0, 0

    def count(self, instruction):
        self.n += 1
        instruction.then_inc(self.semaphore, 1)

    def wait(self, behind=0):
        self.engine.wait_ge(self.semaphore, self.base + (self.n - behind))

    def wait_for(self, instruction):
        self.count(instruction)
        self.wait()


def passes(hi, lo, moving_hi, moving_lo):
    return ((hi, moving_hi), (hi, moving_lo), (lo, moving_hi))


def build(nc, x, wq, wk, wv, wo_t, cols, gate_t, gate_b, expert_t, expert_b, bo, out):
    g_dram = nc.dram_tensor("silu_gate_scratch", [S, D], F32).ap()
    x2, out2 = x[0], out[0]

    ctx = ExitStack()
    with ctx:
        def sb(name, shape, dt=F32, where=ctx, side="left"):
            return where.enter_context(nc.sbuf_tensor(name, shape, dt, side=side))

        def ps(name, shape, where):
            return where.enter_context(nc.psum_tensor(name, shape, F32))

        def sem(name):
            return ctx.enter_context(nc.semaphore(name))

        a_hi = sb("a_hi", [P, KD, D], F32R)
        a_lo = sb("a_lo", [P, KD, D], F32R)
        q_bias = sb("q_bias", [P, KD])
        o_bias = sb("o_bias", [P, D])
        r_all = sb("r_all", [P, NT])
        ident = sb("ident", [P, P])
        r_cur = sb("r_cur", [P, 2, 3])
        q_hi = sb("q_hi", [P, KD, GW], F32R)
        q_lo = sb("q_lo", [P, KD, GW], F32R)
        g_sb = sb("g_sb", [P, 2, GT, D])
        ex_ready = sem("ex_ready")
        r_ready, t_ready, hi_done, lo_done = map(sem, ("r_ready", "t_ready", "hi_done", "lo_done"))
        g_stored = sem("g_stored")

        phase12 = ExitStack()
        vg_hi = sb("vg_hi", [P, KD, D + GC], F32R, phase12, "right")
        vg_lo = sb("vg_lo", [P, KD, D + GC], F32R, phase12, "right")
        ew_hi = sb("ew_hi", [P, KD, E * D], F32R, phase12, "right")
        ew_lo = sb("ew_lo", [P, KD, E * D], F32R, phase12, "right")
        eb_rows = sb("eb_rows", [ROWS, D], F32R, phase12, "right")
        g_bias = sb("g_bias", [P, GT, GC], F32, phase12, "right")
        expert_no = sb("expert_no", [P, E], F32, phase12, "right")
        rstd = sb("rstd", [P, NT], F32, phase12, "right")
        shift = sb("shift", [P, NT], F32, phase12, "right")
        w_cols = sb("w_cols", [P, GT, ROWS], F32R, phase12, "right")
        xn = sb("xn", [P, GT, D], F32, phase12, "right")
        xn_ready = sem("xn_ready")

        xn_hi = sb("xn_hi", [P, KD, S], F32R)
        xn_lo = sb("xn_lo", [P, KD, S], F32R)
        x_in = sb("x_in", [P, 2, GT, D], F32, phase12, "right")
        st_hi = sb("st_hi", [P, 2, KD, GW], F32R, phase12, "right")
        st_lo = sb("st_lo", [P, 2, KD, GW], F32R, phase12, "right")
        ps_x = ps("ps_x", [P, KD, GW], phase12)
        ps_v = ps("ps_v", [P, GT, BANK], phase12)
        ps_y = ps("ps_y", [P, GT, D], phase12)
        xt_ready, xt_hi, xt_lo, kept, ew_low = map(sem, ("xt_ready", "xt_hi", "xt_lo", "kept", "ew_low"))

        def query_half(j, half, dst):
            i = 0
            for k in range(KD):
                hi, lo = (a[:, k, half * P:(half + 1) * P] for a in (a_hi, a_lo))
                toks = bass.ds(j * GW, GW)
                for left, right in passes(hi, lo, xn_hi[:, k, toks], xn_lo[:, k, toks]):
                    mm = nc.tensor.matmul(dst, left, right, start=i == 0, stop=i == 3 * KD - 1)
                    i += 1
            mm.then_inc(t_ready, 1)

        def query_high(half, src):
            nc.scalar.activation(q_hi[:, half, :], src, ACT.Identity, bias=q_bias[:, half:half + 1]
                                 ).then_inc(hi_done, 1)

        def query_low(half, src):
            nc.vector.scalar_tensor_tensor(q_lo[:, half, :], src, q_bias[:, half:half + 1],
                                           q_hi[:, half, :].bitcast(F32), ALU.add, ALU.subtract).then_inc(lo_done, 1)

        def row_terms(tile, par):
            src = r_all[:, bass.ds(tile, 1)]
            for n, factor in enumerate((1.0, 0.5, -1.0)):
                last = nc.vector.tensor_scalar(r_cur[:, par, n:n + 1], src, factor, None, ALU.mult)
            last.then_inc(r_ready, 1)

        def xn_transposes(pe, f):
            pe.wait_ge(xn_ready, f + 1)
            after(pe, xt_lo, f)
            for t in range(GT):
                for k in range(KD):
                    tr = nc.tensor.transpose(ps_x[:, k, t * P:(t + 1) * P], xn[:, t, k * P:(k + 1) * P],
                                             ident[:])
            tr.then_inc(xt_ready, 1)

        def xn_high(act, f, par):
            act.wait_ge(xt_ready, f + 1)
            after(act, ex_ready, 2 * NE * f - 2 * NE)
            after(act, kept, f - 1)
            nc.scalar.copy(st_hi[:, par], ps_x[:]).then_inc(xt_hi, 1)

        def xn_low(dve, f, par):
            dve.wait_ge(xt_hi, f + 1)
            nc.vector.tensor_tensor(st_lo[:, par], ps_x[:], st_hi[:, par].bitcast(F32), ALU.subtract
                                    ).then_inc(xt_lo, 1)

        with nc.Block() as block:
            with ExitStack() as ph:
                wq_sb = sb("wq_sb", [P, KD, D], F32, ph)
                wk_sb = sb("wk_sb", [P, KD, D], F32, ph)
                wv_sb = sb("wv_sb", [P, KD, D], F32, ph)
                wo_sb = sb("wo_sb", [P, KD, D], F32, ph)
                cols_sb = sb("cols_sb", [P, KD, 3], F32, ph)
                bq_wide = sb("bq_wide", [P, KD, P], F32, ph)
                bv_wide = sb("bv_wide", [P, KD, P], F32, ph)
                gb_sb = sb("gb_sb", [1, E], F32, ph)
                bo_sb = sb("bo_sb", [1, D], F32, ph)
                eb = sb("eb", [ROWS, D], F32, ph)
                gw = sb("gw", [P, KD, GC], F32, ph)
                ew = sb("ew", [P, KD, E * D], F32, ph)
                ones = sb("ones", [1, P], F32, ph)
                expert_i = sb("expert_i", [P, E], I32, ph)
                x_all = sb("x_all", [P, NT, D], F32, ph)
                stats = sb("stats", [P, NT, 6], F32, phase12, "right")
                mean = sb("mean", [P, NT], F32, phase12, "right")
                spread = sb("spread", [P, NT], F32, phase12, "right")
                var = sb("var", [P, NT], F32, phase12, "right")
                newton = sb("newton", [P, NT], F32, phase12, "right")
                ps_a = ps("ps_a", [P, KD, D], ph)
                ps_b = ps("ps_b", [P, KD, D], ph)
                ps_o = ps("ps_o", [P, BANK], ph)
                ps_c = ps("ps_c", [P, BANK], ph)
                eb_in = sem("eb_in")
                qk_in, small_in, big_in = sem("qk_in"), sem("small_in"), [sem("big_in0"), sem("big_in1")]
                pool_const, wide_done = sem("pool_const"), sem("wide_done")
                ew_high = sem("ew_high")
                products, w_hi, w_steps = sem("products"), sem("w_hi"), sem("w_steps")
                SMALL = 5
                EW_PARTS = [(k, slice(h, h + E * D // 2)) for k in range(KD) for h in (0, E * D // 2)]
                XPARTS = 4
                TPP = NT // XPARTS
                x_part = [sem(f"x_part{n}") for n in range(XPARTS)]
                ln_steps = [sem("ln_steps0"), sem("ln_steps1")]
                stats_done, shift_ready = sem("stats_done"), sem("shift_ready")

                def load_x(engine, n):
                    engine.dma_start(x_all[:, n * TPP:(n + 1) * TPP, :],
                                     x2[n * TPP * P:(n + 1) * TPP * P, :].rearrange("(t p) d -> p t d", p=P)
                                     ).then_inc(x_part[n], 16)

                def normalise_first(f):
                    for t in range(GT):
                        tile = f * GT + t
                        last = nc.scalar.activation(xn[:, t, :], x_all[:, tile, :], ACT.Identity,
                                                    scale=rstd[:, tile:tile + 1], bias=shift[:, tile:tile + 1])
                    last.then_inc(xn_ready, 1)

                def ew_low_part(engine, unit, n):
                    k, half = EW_PARTS[n]
                    engine.wait_ge(ew_high, n + 1)
                    unit.tensor_tensor(ew_lo[:, k, half], ew[:, k, half], ew_hi[:, k, half].bitcast(F32), ALU.subtract
                                       ).then_inc(ew_low, 1)

                def statistics(dve, first_tile, last_tile):
                    dve.wait_ge(x_part[first_tile // TPP], 16)
                    for tile in range(first_tile, last_tile):
                        nc.vector.bn_stats(stats[:, tile, :], x_all[:, tile, :]).then_inc(stats_done, 1)

                def layer_norm_terms(engine, unit, step, first_tile, last_tile):
                    tiles = slice(first_tile, last_tile)
                    even, odd = stats[:, tiles, 1], stats[:, tiles, 4]
                    neg_mean, half_diff, v, g, r = (a[:, tiles] for a in (mean, spread, var, newton, rstd))
                    engine.wait_ge(stats_done, last_tile)
                    unit.tensor_tensor(neg_mean, even, odd, ALU.add)
                    unit.tensor_tensor(half_diff, even, odd, ALU.subtract)
                    step.wait_for(unit.tensor_tensor(v, stats[:, tiles, 2], stats[:, tiles, 5], ALU.add))
                    unit.tensor_scalar(neg_mean, neg_mean, -0.5, None, ALU.mult)
                    unit.tensor_scalar(half_diff, half_diff, 0.5, None, ALU.mult)
                    step.wait_for(unit.tensor_scalar(v, v, 1.0 / D, EPS, ALU.mult, ALU.add))
                    step.wait_for(unit.tensor_tensor(half_diff, half_diff, half_diff, ALU.mult))
                    step.wait_for(unit.tensor_tensor(v, v, half_diff, ALU.add))
                    step.wait_for(unit.tensor_scalar(r.bitcast(I32), v.bitcast(I32), -0.5, RSQRT_MAGIC,
                                                     ALU.mult, ALU.add))
                    for _ in range(3):
                        step.wait_for(unit.tensor_tensor(g, r, r, ALU.mult))
                        step.wait_for(unit.tensor_tensor(g, g, v, ALU.mult))
                        step.wait_for(unit.tensor_scalar(g, g, -0.5, 1.5, ALU.mult, ALU.add))
                        step.wait_for(unit.tensor_tensor(r, r, g, ALU.mult))
                    unit.tensor_tensor(shift[:, tiles], neg_mean, r, ALU.mult).then_inc(shift_ready, 1)

                @block.sync
                def _(sp):
                    for tile, src in ((cols_sb, cols), (wq_sb, wq), (wk_sb, wk)):
                        sp.dma_start(tile[:], src.rearrange("(k p) n -> p k n", p=P)).then_inc(qk_in, 16)
                    for tile, src in ((wv_sb, wv), (wo_sb, wo_t)):
                        sp.dma_start(tile[:], src.rearrange("(k p) n -> p k n", p=P)).then_inc(small_in, 16)
                    for k in range(KD):
                        sp.dma_start(ew[:, k, :], expert_t[k * P:(k + 1) * P, :]).then_inc(big_in[k], 16)
                    for n in range(1, XPARTS):
                        load_x(sp, n)

                @block.gpsimd
                def _(pool):
                    nc.gpsimd.memset(ident[:], 0.0).then_inc(pool_const, 1)
                    nc.gpsimd.memset(ones[:], 1.0).then_inc(pool_const, 1)
                    nc.gpsimd.iota(expert_i[:], [[1, E]], base=0, channel_multiplier=0).then_inc(pool_const, 1)
                    pool.wait_ge(pool_const, 3)
                    nc.gpsimd.affine_select(out=ident[:], in_=ident[:], compare_op=ALU.not_equal, fill=1.0, base=0,
                                            pattern=[[-1, P]], channel_multiplier=1).then_inc(pool_const, 1)
                    for n in (0, 1, 2):
                        ew_low_part(pool, nc.gpsimd, n)

                @block.tensor
                def _(pe):
                    for acc, left, right, loaded, loads in (
                            (ps_a, wq_sb, wk_sb, qk_in, 3), (ps_b, wv_sb, wo_sb, small_in, SMALL)):
                        pe.wait_ge(loaded, 16 * loads)
                        for h in range(KD):
                            for k in range(KD):
                                mm = nc.tensor.matmul(acc[:, h, :], left[:, k, h * P:(h + 1) * P], right[:, k, :],
                                                      start=k == 0, stop=k == KD - 1)
                        mm.then_inc(products, 1)
                    for n, (left, col) in enumerate(((wk_sb, 0), (wq_sb, 1))):
                        for h in range(KD):
                            for k in range(KD):
                                nc.tensor.matmul(ps_c[:, n * KD + h:n * KD + h + 1], left[:, k, h * P:(h + 1) * P],
                                                 cols_sb[:, k, col:col + 1], start=k == 0, stop=k == KD - 1)
                    pe.wait_ge(pool_const, 4)
                    nc.tensor.matmul(ps_c[:, 8:8 + E], ones[:], gb_sb[:], start=True, stop=True)
                    pe.wait_ge(wide_done, 2)
                    for k in range(KD):
                        mm = nc.tensor.matmul(ps_c[:, 8 + E:9 + E], bq_wide[:, k, :], cols_sb[:, k, 1:2],
                                              start=k == 0, stop=k == KD - 1)
                    mm.then_inc(products, 1)
                    xn_transposes(pe, 0)
                    for k in range(KD):
                        nc.tensor.matmul(ps_o[:, 0:D], bv_wide[:, k, :], wo_sb[:, k, :], start=k == 0, stop=False)
                    nc.tensor.matmul(ps_o[:, 0:D], ones[:], bo_sb[:], start=False, stop=True).then_inc(products, 1)

                @block.scalar
                def _(act):
                    load_x(act, 0)
                    act.dma_start(gw[:, :, 0:E], gate_t.rearrange("(k p) n -> p k n", p=P)).then_inc(small_in, 16)
                    act.dma_start(gb_sb[:], gate_b).then_inc(small_in, 16)
                    act.dma_start(bo_sb[:], bo).then_inc(small_in, 16)
                    act.wait_ge(w_steps, 2)
                    for row in range(0, ROWS, ROW_STEP):
                        act.dma_start(eb[row:row + E, :], expert_b).then_inc(eb_in, 16)

                    def expert_high(n):
                        k, half = EW_PARTS[n]
                        act.wait_ge(big_in[k], 16)
                        nc.scalar.copy(ew_hi[:, k, half], ew[:, k, half]).then_inc(ew_high, 1)

                    act.wait_ge(products, 1)
                    nc.scalar.copy(a_hi[:], ps_a[:]).then_inc(w_hi, 1)
                    expert_high(0)
                    act.wait_ge(products, 2)
                    nc.scalar.copy(vg_hi[:, :, 0:D], ps_b[:]).then_inc(w_hi, 1)
                    act.wait_ge(shift_ready, 1)
                    normalise_first(0)
                    expert_high(1)
                    xn_high(act, 0, 0)
                    expert_high(2)
                    expert_high(3)

                @block.vector
                def _(dve):
                    nc.vector.memset(gw[:, :, E:GC], 0.0).then_inc(w_steps, 1)
                    nc.vector.memset(g_bias[:], 0.0)
                    nc.vector.memset(w_cols[:].bitcast(F32), 0.0)
                    nc.vector.memset(eb[:], 0.0).then_inc(w_steps, 1)
                    dve.wait_ge(pool_const, 3)
                    nc.vector.tensor_copy(expert_no[:], expert_i[:])
                    statistics(dve, 0, TPP)
                    dve.wait_ge(qk_in, 16 * 3)
                    nc.vector.tensor_copy(bq_wide[:], cols_sb[:, :, 0:1].broadcast_to([P, KD, P])
                                          ).then_inc(wide_done, 1)
                    nc.vector.tensor_copy(bv_wide[:], cols_sb[:, :, 2:3].broadcast_to([P, KD, P])
                                          ).then_inc(wide_done, 1)
                    layer_norm_terms(dve, nc.vector, Steps(dve, ln_steps[0]), 0, TPP)
                    dve.wait_ge(w_hi, 1)
                    nc.vector.tensor_tensor(a_lo[:], ps_a[:], a_hi[:].bitcast(F32), ALU.subtract)
                    dve.wait_ge(w_hi, 2)
                    nc.vector.tensor_tensor(vg_lo[:, :, 0:D], ps_b[:], vg_hi[:, :, 0:D].bitcast(F32), ALU.subtract)
                    dve.wait_ge(products, 3)
                    dve.wait_ge(w_steps, 2)
                    nc.vector.tensor_copy(q_bias[:], ps_c[:, 0:KD])
                    nc.vector.tensor_copy(gw[:, :, E], ps_c[:, KD:2 * KD]).then_inc(w_steps, 1)
                    for t in range(GT):
                        nc.vector.tensor_copy(g_bias[:, t, 0:E + 1], ps_c[:, 8:9 + E])
                    dve.wait_ge(w_steps, 3)
                    nc.vector.tensor_copy(vg_hi[:, :, D:], gw[:]).then_inc(w_steps, 1)
                    dve.wait_ge(w_steps, 4)
                    nc.vector.tensor_tensor(vg_lo[:, :, D:], gw[:], vg_hi[:, :, D:].bitcast(F32), ALU.subtract)
                    xn_low(dve, 0, 0)
                    dve.wait_ge(eb_in, 16 * 3)
                    nc.vector.tensor_copy(eb_rows[:], eb[:]).then_inc(w_steps, 1)
                    dve.wait_ge(w_steps, 5)
                    low = slice(ROW_STEP, ROW_STEP + E)
                    nc.vector.tensor_tensor(eb_rows[low, :], eb[low, :], eb_rows[low, :].bitcast(F32), ALU.subtract)
                    dve.wait_ge(products, 4)
                    nc.vector.tensor_copy(o_bias[:], ps_o[:, 0:D])
                    statistics(dve, TPP, TPP + TPP // 2)
                    ew_low_part(dve, nc.vector, 3)

            vals = sb("vals", [P, NT, 2 * D], F32R)

            with ExitStack() as ph:
                logits = sb("logits", [P, GT, GC], F32, ph)
                top = sb("top", [P, GT, 8], F32, ph)
                which = sb("which", [P, GT, 8], U32, ph)
                ldiff = sb("ldiff", [P, GT, E], F32, ph)
                gexp = sb("gexp", [P, GT, E], F32, ph)
                gsum = sb("gsum", [P, GT, 1], F32, ph)
                ginv = sb("ginv", [P, GT, 1], F32, ph)
                first = sb("first", [P, GT, E], F32, ph)
                second = sb("second", [P, GT, E], F32, ph)
                wts = sb("wts", [P, 2, GT, E], F32, ph)
                wt_t = sb("wt_t", [ROWS, GW], F32R, ph)
                acc = sb("acc", [P, 2, GT, D], F32, ph)
                tnh = sb("tnh", [P, GT, D], F32, ph)
                ps_e = [ps(f"ps_e{n}", [P, BANK], ph) for n in range(NE)]
                VG = D + GC
                WT = BANK - P

                x_loaded = [sem("x_loaded0"), sem("x_loaded1")]
                gate_steps, ldiff_ready, gexp_ready = map(sem, ("gate_steps", "ldiff_ready", "gexp_ready"))
                w_ready, w_split, wt_ready, wt_sb_ready = map(sem, ("w_ready", "w_split", "wt_ready", "wt_sb_ready"))
                yb_ready, y_done, vg_ready, v_hi, v_lo = map(sem, ("yb_ready", "y_done", "vg_ready", "v_hi", "v_lo"))
                ex_used, tnh_ready, g_ready = map(sem, ("ex_used", "tnh_ready", "g_ready"))
                mix_steps = sem("mix_steps")

                def bodies(engine, body):
                    body(0)
                    with engine.Fori(1, NG // 2 - 1) as j:
                        body(j)
                    body(NG // 2 - 1)

                @block.sync
                def _(sp):
                    def load(f, par):
                        after(sp, xn_ready, f - 1)
                        sp.dma_start(x_in[:, par], x2[bass.ds(f * GW, GW), :].rearrange("(t p) d -> p t d", p=P)
                                     ).then_inc(x_loaded[par], 16)

                    def store(u, par):
                        sp.wait_ge(g_ready, u + 1)
                        sp.dma_start(g_dram[bass.ds(u * GW, GW), :].rearrange("(t p) d -> p t d", p=P),
                                     g_sb[:, par]).then_inc(g_stored, 16)

                    def body(j):
                        for p in range(2):
                            u = 2 * j + p
                            if there(u + 2, NG):
                                load(u + 2, p)
                            if there(u - 1, NG):
                                store(u - 1, 1 - p)

                    bodies(sp, body)
                    store(NG - 1, (NG - 1) % 2)

                @block.gpsimd
                def _(pool):
                    def keep(f, par):
                        after_both(pool, xt_lo, f + 1, pool_const, 4)
                        nc.gpsimd.tensor_copy(xn_hi[:, :, bass.ds(f * GW, GW)], st_hi[:, par].bitcast(F32))
                        nc.gpsimd.tensor_copy(xn_lo[:, :, bass.ds(f * GW, GW)], st_lo[:, par].bitcast(F32)
                                              ).then_inc(kept, 1)

                    def body(j):
                        for p in range(2):
                            if there(2 * j + p + 1, NG):
                                keep(2 * j + p + 1, 1 - p)
                            if isinstance(j, int) and 2 * j + p == 1:
                                layer_norm_terms(pool, nc.gpsimd, Steps(pool, ln_steps[1]), TPP, NT)

                    keep(0, 0)
                    bodies(pool, body)

                @block.tensor
                def _(pe):
                    def values_gates(f, par):
                        pe.wait_ge(xt_lo, f + 1)
                        after(pe, v_lo, f)
                        after(pe, wt_sb_ready, f)
                        for t in range(GT):
                            n = 0
                            for k in range(KD):
                                hi, lo = (s[:, par, k, t * P:(t + 1) * P] for s in (st_hi, st_lo))
                                for left, right in passes(hi, lo, vg_hi[:, k, :], vg_lo[:, k, :]):
                                    mm = nc.tensor.matmul(ps_v[:, t, 0:VG], left, right, start=n == 0,
                                                          stop=n == 3 * KD - 1)
                                    n += 1
                        mm.then_inc(vg_ready, 1)

                    def weights_t(u):
                        pe.wait_ge(w_split, u + 1)
                        pe.wait_ge(v_lo, u + 1)
                        for t in range(GT):
                            tr = nc.tensor.transpose(ps_v[0:ROWS, t, WT:BANK], w_cols[:, t, :].bitcast(F32), ident[:])
                        tr.then_inc(wt_ready, 1)

                    def bias_mix(u):
                        pe.wait_ge(wt_sb_ready, u + 1)
                        after(pe, y_done, u)
                        for t in range(GT):
                            mm = nc.tensor.matmul(ps_y[:, t, :], wt_t[:, t * P:(t + 1) * P], eb_rows[:],
                                                  start=True, stop=True)
                        mm.then_inc(yb_ready, 1)

                    def expert(u, par, m):
                        b, t, bank = m // GT, m % GT, m % NE
                        after(pe, ex_used, u * GT * NE + (m - NE + 1))
                        n = 0
                        for k in range(KD):
                            hi, lo = (a[:, par, k, t * P:(t + 1) * P] for a in (st_hi, st_lo))
                            columns = slice(b * BANK, (b + 1) * BANK)
                            for left, right in passes(hi, lo, ew_hi[:, k, columns], ew_lo[:, k, columns]):
                                mm = nc.tensor.matmul(ps_e[bank][:], left, right, start=n == 0, stop=n == 3 * KD - 1)
                                n += 1
                        mm.then_inc(ex_ready, 1)

                    def body(j):
                        for p in range(2):
                            u, f = 2 * j + p, 2 * j + p + 1
                            more = there(f, NG)
                            if more:
                                xn_transposes(pe, f)
                            expert(u, p, 0)
                            early = isinstance(u, int) and u == 0
                            if early:
                                expert(u, p, 1)
                            weights_t(u)
                            if not early:
                                expert(u, p, 1)
                            if more:
                                values_gates(f, 1 - p)
                            else:
                                pe.wait_ge(kept, 1)
                                for half in range(KD):
                                    query_half(0, half, ps_x[:, half, :])
                            bias_mix(u)
                            for m in range(2, GT * NE):
                                expert(u, p, m)

                    values_gates(0, 0)
                    pe.wait_ge(ew_low, len(EW_PARTS))
                    bodies(pe, body)

                @block.scalar
                def _(act):
                    def normalise(f, par, uses):
                        after(act, xt_ready, f)
                        early = isinstance(f, int) and (f + 1) * GT <= TPP
                        after_both(act, x_loaded[par], 16 * uses, shift_ready, 1 if early else 2)
                        for t in range(GT):
                            tile = bass.ds(f * GT + t, 1)
                            last = nc.scalar.activation(xn[:, t, :], x_in[:, par, t, :], ACT.Identity,
                                                        scale=rstd[:, tile], bias=shift[:, tile])
                        last.then_inc(xn_ready, 1)

                    def weights_t(u):
                        act.wait_ge(wt_ready, u + 1)
                        after(act, yb_ready, u)
                        nc.scalar.copy(wt_t[:].rearrange("e (t p) -> e t p", p=P), ps_v[0:ROWS, :, WT:BANK]
                                       ).then_inc(wt_sb_ready, 1)

                    def split_v(f):
                        after_both(act, vg_ready, f + 1, w_hi, 2)
                        nc.scalar.copy(vals[:, bass.ds(f * GT, GT), 0:D], ps_v[:, :, 0:D]).then_inc(v_hi, 1)

                    def gate_exp(f):
                        act.wait_ge(ldiff_ready, f + 1)
                        nc.scalar.activation(gexp[:], ldiff[:], ACT.Exp).then_inc(gexp_ready, 1)

                    def tanh_acc(u, par):
                        act.wait_ge(y_done, u + 1)
                        after(act, g_ready, u)
                        nc.scalar.activation(tnh[:], acc[:, par], ACT.Tanh).then_inc(tnh_ready, 1)

                    def body(j):
                        for p in range(2):
                            u, f = 2 * j + p, 2 * j + p + 1
                            if there(f, NG):
                                xn_high(act, f, 1 - p)
                            weights_t(u)
                            if there(u - 1, NG):
                                tanh_acc(u - 1, 1 - p)
                            if there(u + 2, NG):
                                normalise(u + 2, p, j + 1)
                            if there(f, NG):
                                split_v(f)
                                gate_exp(f)
                            else:
                                act.wait_ge(t_ready, KD)
                                for half in range(KD):
                                    query_high(half, ps_x[:, half, :])

                    split_v(0)
                    act.wait_ge(xt_ready, 1)
                    normalise_first(1)
                    gate_exp(0)
                    bodies(act, body)
                    tanh_acc(NG - 1, (NG - 1) % 2)

                @block.vector
                def _(dve):
                    mix = Steps(dve, mix_steps)
                    gate = Steps(dve, gate_steps)

                    def gate_logits(f):
                        dve.wait_ge(v_hi, f + 1)
                        gate.count(nc.vector.tensor_tensor(logits[:], ps_v[:, :, D:VG], g_bias[:], ALU.add))

                    def gate_order(f):
                        gate.wait()
                        nc.vector.tensor_scalar(r_all[:, bass.ds(f * GT, GT)], logits[:, :, E], 1.0, None, ALU.mult)
                        for t in range(GT):
                            last = nc.vector.max(top[:, t, :], logits[:, t, 0:E])
                        gate.count(last)

                    def gate_experts(f):
                        gate.wait()
                        nc.vector.tensor_tensor(ldiff[:], logits[:, :, 0:E], top[:, :, 0:1].broadcast_to([P, GT, E]),
                                                ALU.subtract).then_inc(ldiff_ready, 1)
                        for t in range(GT):
                            last = nc.vector.max_index(which[:, t, :], top[:, t, :], logits[:, t, 0:E])
                        gate.count(last)

                    def gate_two(f):
                        dve.wait_ge(gexp_ready, f + 1)
                        gate.count(nc.vector.tensor_reduce(gsum[:], gexp[:], AX.X, ALU.add))
                        gate.wait()
                        for t in range(GT):
                            for n, pick in enumerate((first, second)):
                                last = nc.vector.scalar_tensor_tensor(pick[:, t, :], expert_no[:], which[:, t, n:n + 1],
                                                                      gexp[:, t, :], ALU.is_equal, ALU.mult)
                        nc.vector.reciprocal(ginv[:], gsum[:])
                        gate.count(last)

                    def gate_sum(f):
                        gate.wait()
                        gate.count(nc.vector.tensor_tensor(first[:], first[:], second[:], ALU.add))

                    def gate_weights(f, par):
                        gate.wait()
                        nc.vector.scalar_tensor_tensor(wts[:, par], first[:], 0.5, ginv[:].broadcast_to([P, GT, E]),
                                                       ALU.mult, ALU.mult).then_inc(w_ready, 1)

                    def gate_high(f, par):
                        dve.wait_ge(w_ready, f + 1)
                        after(dve, wt_ready, f)
                        for part in (0, 1):
                            col = part * ROW_STEP
                            last = nc.vector.tensor_copy(w_cols[:, :, col:col + E], wts[:, par])
                        gate.count(last)

                    def gate_low(f, par):
                        gate.wait()
                        nc.vector.tensor_tensor(w_cols[:, :, 2 * ROW_STEP:2 * ROW_STEP + E], wts[:, par],
                                                w_cols[:, :, 0:E].bitcast(F32), ALU.subtract).then_inc(w_split, 1)

                    def split_v(f):
                        nc.vector.tensor_tensor(vals[:, bass.ds(f * GT, GT), D:2 * D], ps_v[:, :, 0:D],
                                                vals[:, bass.ds(f * GT, GT), 0:D].bitcast(F32), ALU.subtract
                                                ).then_inc(v_lo, 1)

                    def expert(u, par, n):
                        b, half, t = n // (2 * GT), n // GT % 2, n % GT
                        e, m = 2 * b + half, b * GT + t
                        if n == 0:
                            dve.wait_ge(w_ready, u + 1)
                        if half == 0:
                            dve.wait_ge(ex_ready, u * GT * NE + (m + 1))
                            if b > 0:
                                dve.wait_ge(ex_used, u * GT * NE + (m - GT + 1))
                        else:
                            mix.wait(behind=GT - 1 - t)
                        a, y, w = acc[:, par, t, :], ps_e[m % NE][:, half * D:(half + 1) * D], wts[:, par, t, e:e + 1]
                        if e == 0:
                            new = nc.vector.tensor_scalar(a, y, w, None, ALU.mult)
                        else:
                            new = nc.vector.scalar_tensor_tensor(a, y, w, a, ALU.mult, ALU.add)
                        if half == 0:
                            mix.count(new)
                        else:
                            new.then_inc(ex_used, 1)

                    def add_bias(u, par):
                        dve.wait_ge(yb_ready, u + 1)
                        dve.wait_ge(ex_used, u * 2 * NE + 2 * NE)
                        nc.vector.tensor_tensor(acc[:, par], ps_y[:], acc[:, par], ALU.add).then_inc(y_done, 1)

                    def silu(u, par):
                        dve.wait_ge(tnh_ready, u + 1)
                        after(dve, g_stored, 16 * u)
                        nc.vector.scalar_tensor_tensor(g_sb[:, par], tnh[:], 1.0, acc[:, par], ALU.add, ALU.mult
                                                       ).then_inc(g_ready, 1)

                    def body(j):
                        for p in range(2):
                            u, f = 2 * j + p, 2 * j + p + 1
                            more, earlier = there(f, NG), there(u - 1, NG)
                            if earlier:
                                add_bias(u - 1, 1 - p)
                            if more:
                                xn_low(dve, f, 1 - p)
                            for n in range(GT * E):
                                expert(u, p, n)
                                if n == 1 and earlier:
                                    silu(u - 1, 1 - p)
                                if n == 3 and more:
                                    gate_logits(f)
                                if n == 4 and more:
                                    gate_order(f)
                                if n == 5 and more:
                                    split_v(f)
                                if n == 6 and more:
                                    gate_experts(f)
                                if n == 8 and more:
                                    gate_two(f)
                                if n == 9 and more:
                                    gate_sum(f)
                                if n == 10 and more:
                                    gate_weights(f, 1 - p)
                                if n == 11 and more:
                                    gate_high(f, 1 - p)
                                if n == 12 and more:
                                    gate_low(f, 1 - p)
                                if n == 8 and not more:
                                    dve.wait_ge(hi_done, KD)
                                    for half in range(KD):
                                        query_low(half, ps_x[:, half, :])
                                    row_terms(0, 0)
                                if isinstance(u, int) and u < 2:
                                    tile = {(0, 4): 12, (0, 11): 16, (1, 3): 20, (1, 7): 24, (1, 11): 28}.get((u, n))
                                    if tile:
                                        statistics(dve, tile, tile + TPP // 2)

                    gate_logits(0)
                    gate_order(0)
                    gate_experts(0)
                    split_v(0)
                    gate_two(0)
                    gate_sum(0)
                    gate_weights(0, 0)
                    gate_high(0, 0)
                    gate_low(0, 0)
                    steps = (mix, gate)
                    ahead = [s.n for s in steps]
                    body(0)
                    per_body = [s.n - n for s, n in zip(steps, ahead)]
                    with dve.Fori(1, NG // 2 - 1) as j:
                        for s, n, by in zip(steps, ahead, per_body):
                            s.base, s.n = j * by, n
                        body(j)
                        assert [s.n for s in steps] == [n + by for n, by in zip(ahead, per_body)]
                    for s, n, by in zip(steps, ahead, per_body):
                        s.base, s.n = 0, n + by * (NG // 2 - 1)
                    body(NG // 2 - 1)
                    add_bias(NG - 1, (NG - 1) % 2)
                    silu(NG - 1, (NG - 1) % 2)
            phase12.close()

            with ExitStack() as ph:
                ring = sb("ring", [P, CPB, CH], F32, ph)
                th = sb("th", [P, 2, CH], F32, ph)
                tz = sb("tz", [P, 2, CH], F32, ph)
                p_hi = sb("p_hi", [P, 2, BANK], F32R, ph)
                p_lo = sb("p_lo", [P, 2, BANK], F32R, ph)
                cmax = sb("cmax", [P, 2, CPT], F32, ph)
                nmax = sb("nmax", [P, 2], F32, ph)
                e_bias = sb("e_bias", [P, 2], F32, ph)
                csum = sb("csum", [P, 2, CPT], F32, ph)
                rsum = sb("rsum", [P, 2], F32, ph)
                rinv = sb("rinv", [P, 2], F32, ph)
                o_lo = sb("o_lo", [P, D], F32, ph)
                att = sb("att", [P, 2, D], F32, ph)
                x_in3 = sb("x_in3", [P, 2, D], F32, ph)
                g_in3 = sb("g_in3", [P, 2, D], F32, ph)
                y_out = g_sb[:, 0]
                ps_s = ps("ps_s", [P, 2, CH], ph)
                ps_t = ps("ps_t", [P, 2, BANK], ph)
                ps_o3 = ps("ps_o3", [P, 2, 2 * D], ph)

                xg_loaded = [sem("xg_loaded0"), sem("xg_loaded1")]
                y_stored = [sem("y_stored0"), sem("y_stored1")]
                scores, tanh_done, a_done, b_done = map(sem, ("scores", "tanh_done", "a_done", "b_done"))
                max_done = sem("max_done")
                nmax_done, bias_ready, exp_done, pv_done = map(sem, ("nmax_done", "bias_ready", "exp_done", "pv_done"))
                rsum_done, rinv_ready = sem("rsum_done"), sem("rinv_ready")
                o_lo_ready, out_read = sem("o_lo_ready"), sem("out_read")
                fin_steps, y_ready = sem("fin_steps"), sem("y_ready")

                PER_BODY = 2 * CPB + KD

                def t_use(j, c, half):
                    q_uses = 2 if not isinstance(j, int) or j < NB else 2 - KD
                    before = 0
                    if c < 0:
                        c, before = c + CPB, PER_BODY
                    return j * PER_BODY + (2 * (c - T_LAG) + half + q_uses - before)

                def q_use(j, half):
                    if isinstance(j, int) and j == 0:
                        return half
                    return j * PER_BODY + (t_use(-1, CPB - 1, 1) + 1 + half)

                def bodies3(engine, body):
                    body(0)
                    body(1)
                    with engine.Fori(2, NB - 1) as j:
                        body(j)
                    body(NB - 1)
                    body(NB)

                @block.sync
                def _(sp):
                    def load(i, par):
                        after(sp, y_ready, i - 1)
                        if isinstance(i, int) and i == 0:
                            sp.wait_ge(g_stored, 16 * NG)
                            sp.wait_ge(scores, 1)
                        rows = bass.ds(i * P, P)
                        sp.dma_start(x_in3[:, par], x2[rows, :]).then_inc(xg_loaded[par], 16)
                        sp.dma_start(g_in3[:, par], g_dram[rows, :]).then_inc(xg_loaded[par], 16)

                    def body(j):
                        for p in range(2):
                            if there(2 * j - 2 + p, NT):
                                sp.wait_ge(y_ready, 2 * j - 1 + p)
                                sp.dma_start(out2[bass.ds((2 * j - 2 + p) * P, P), :], y_out[:, p]
                                             ).then_inc(y_stored[p], 16)
                            if there(2 * j + p, NT):
                                load(2 * j + p, p)

                    bodies3(sp, body)
                    for p in range(2):
                        sp.wait_ge(y_stored[p], 16 * NT // 2)

                @block.tensor
                def _(pe):
                    def queries(j):
                        for half in range(KD):
                            n, bank = q_use(j, half), half
                            after(pe, lo_done, n - 1)
                            query_half(j, half, ps_t[:, bank, 0:GW])

                    def score(c, bank):
                        i = 0
                        keys = slice((c % CPT) * CH + bank * BANK, (c % CPT) * CH + (bank + 1) * BANK)
                        row = slice(c // CPT * P, (c // CPT + 1) * P)
                        for k in range(KD):
                            for left, right in passes(q_hi[:, k, row], q_lo[:, k, row],
                                                      xn_hi[:, k, keys], xn_lo[:, k, keys]):
                                mm = nc.tensor.matmul(ps_s[:, c % 2, bank * BANK:(bank + 1) * BANK], left, right,
                                                      start=i == 0, stop=i == 3 * KD - 1)
                                i += 1
                        return mm

                    def transposes(j, c, half):
                        n = t_use(j, c, half)
                        after(pe, lo_done, n - 1)
                        for b in range(BANK // P):
                            key = half * BANK + b * P
                            tr = nc.tensor.transpose(ps_t[:, half, b * P:(b + 1) * P],
                                                     ring[:, (c - T_LAG) % CPB, key:key + P], ident[:])
                        tr.then_inc(t_ready, 1)

                    def weigh(j, c, half):
                        h = (c - T_LAG) % CPB
                        first = h % CPT == 0 and half == 0
                        if first:
                            tile = 2 * j + (c - T_LAG) // CPT
                            after(pe, out_read, tile - 1)
                        pe.wait_ge(lo_done, t_use(j, c, half) + 1)
                        o = ps_o3[:, h // CPT]
                        for b in range(BANK // P):
                            key_tile = (h % CPT) * (CH // P) + half * (BANK // P) + b
                            hi, lo = (p[:, half, b * P:(b + 1) * P] for p in (p_hi, p_lo))
                            end = h % CPT == CPT - 1 and half == 1 and b == BANK // P - 1
                            nc.tensor.matmul(o[:], hi, vals[:, key_tile, :], start=first and b == 0, stop=False,
                                             skip_group_check=True)
                            mm = nc.tensor.matmul(o[:, 0:D], lo, vals[:, key_tile, 0:D], start=False, stop=end,
                                                  skip_group_check=True)
                        mm.then_inc(pv_done, 1)

                    def body(j):
                        for c in range(CPB):
                            s = CPB * j + c
                            make, use = there(s, NB * CPB), there(s - T_LAG, NB * CPB)
                            used = there(s - T_LAG - 1, NB * CPB)
                            if isinstance(s, int) and s == 1:
                                pe.wait_ge(y_done, NG)
                            if make and c == 0:
                                q_wait = q_use(j, 1) + 1
                            if make and c > 0:
                                after(pe, a_done, s - 1)
                                score(c, 0)
                            if use:
                                pe.wait_ge(exp_done, s - T_LAG + 1)
                                transposes(j, c, 0)
                                transposes(j, c, 1)
                            if used:
                                weigh(j - 1 if c == 0 else j, (c - 1) % CPB, 1)
                            if make:
                                if c == 0:
                                    pe.wait_ge(lo_done, q_wait)
                                    after(pe, a_done, s - 1)
                                    score(c, 0)
                                score(c, 1).then_inc(scores, 1)
                            if c == CPB - 1 and there(j + 1, NB):
                                queries(j + 1)
                            if use:
                                weigh(j, c, 0)

                    pe.wait_ge(kept, NG)
                    bodies3(pe, body)

                @block.scalar
                def _(act):
                    def split_p(j, c, half):
                        n = t_use(j, c, half)
                        act.wait_ge(t_ready, n + 1)
                        after(act, pv_done, 2 * CPB * j + 2 * (c - T_LAG) + half - 1)
                        nc.scalar.copy(p_hi[:, half], ps_t[:, half]).then_inc(hi_done, 1)

                    def split_q(j):
                        for half in range(KD):
                            act.wait_ge(t_ready, q_use(j, half) + 1)
                            query_high(half, ps_t[:, half, 0:GW])

                    def body(j):
                        for c in range(CPB):
                            s = CPB * j + c
                            if there(s - EXP_LAG, NB * CPB):
                                e = (c - EXP_LAG) % CPB
                                tile = 2 * j + (c - EXP_LAG) // CPT
                                if e % CPT == 0:
                                    act.wait_ge(bias_ready, tile + 1)
                                    after(act, rinv_ready, tile - 1)
                                nc.scalar.activation(ring[:, e], ring[:, e], ACT.Exp, scale=0.1,
                                                     bias=e_bias[:, e // CPT:e // CPT + 1],
                                                     accum_out=csum[:, e // CPT, e % CPT:e % CPT + 1]
                                                     ).then_inc(exp_done, 1)
                            if there(s - T_LAG, NB * CPB):
                                split_p(j, c, 0)
                                split_p(j, c, 1)
                            if c % CPT == 2 and there(s - 2 * CPT - 2, NB * CPB):
                                i, par = 2 * j + c // CPT - 2, c // CPT
                                act.wait_ge(pv_done, i * 2 * CPT + 2 * CPT)
                                act.wait_ge(rinv_ready, i + 1)
                                after(act, out_read, i)
                                nc.scalar.activation(o_lo[:], ps_o3[:, par, D:2 * D], ACT.Copy,
                                                     scale=rinv[:, par:par + 1]).then_inc(o_lo_ready, 1)
                            if c == CPB - 1 and there(j + 1, NB):
                                split_q(j + 1)
                            if there(s, NB * CPB):
                                act.wait_ge(scores, s + 1)
                                after(act, b_done, s - 1)
                                if c % CPT == 0:
                                    act.wait_ge(r_ready, 2 * j + c // CPT + 1)
                                nc.scalar.activation(th[:, c % 2], ps_s[:, c % 2], ACT.Tanh, scale=0.5,
                                                     bias=r_cur[:, c // CPT, 1:2])
                                nc.scalar.activation(tz[:, c % 2], ps_s[:, c % 2], ACT.Tanh,
                                                     bias=r_cur[:, c // CPT, 0:1]).then_inc(tanh_done, 1)

                    bodies3(act, body)

                @block.vector
                def _(dve):
                    def split_p(j, c, half):
                        dve.wait_ge(hi_done, t_use(j, c, half) + 1)
                        nc.vector.tensor_tensor(p_lo[:, half], ps_t[:, half], p_hi[:, half].bitcast(F32), ALU.subtract
                                                ).then_inc(lo_done, 1)

                    def split_q(j):
                        for half in range(KD):
                            dve.wait_ge(hi_done, q_use(j, half) + 1)
                            query_low(half, ps_t[:, half, 0:GW])

                    def body(j):
                        for c in range(CPB):
                            s = CPB * j + c
                            k = (c - 1) % CPB
                            tile, par = 2 * j + (c - 1) // CPT, k // CPT
                            score_there, p_there = there(s - 1, NB * CPB), there(s - T_LAG, NB * CPB)
                            if score_there:
                                dve.wait_ge(tanh_done, s)
                                nc.vector.scalar_tensor_tensor(th[:, k % 2], ps_s[:, k % 2], r_cur[:, par, 2:3],
                                                               th[:, k % 2], ALU.max, ALU.add).then_inc(a_done, 1)
                            if p_there:
                                split_p(j, c, 0)
                            if score_there:
                                dve.wait_ge(a_done, s)
                                if there(s - 1 - CPB, NB * CPB):
                                    dve.wait_ge(t_ready, t_use(j, c - 1 - CPB + T_LAG, 1) + 1)
                                nc.vector.scalar_tensor_tensor(ring[:, k], tz[:, k % 2], 1.5, th[:, k % 2],
                                                               ALU.mult, ALU.add).then_inc(b_done, 1)
                            if p_there:
                                split_p(j, c, 1)
                            if score_there:
                                dve.wait_ge(b_done, s)
                                nc.vector.tensor_reduce(cmax[:, par, k % CPT:k % CPT + 1], ring[:, k], AX.X, ALU.max
                                                        ).then_inc(max_done, 1)
                                if k % CPT == CPT - 1:
                                    dve.wait_ge(max_done, s)
                                    nc.vector.tensor_reduce(nmax[:, par:par + 1], cmax[:, par], AX.X, ALU.max,
                                                            negate=True).then_inc(nmax_done, 1)
                                    dve.wait_ge(nmax_done, tile + 1)
                                    after(dve, exp_done, CPT * (tile - 1))
                                    nc.vector.tensor_scalar(e_bias[:, par:par + 1], nmax[:, par:par + 1], 0.1, None,
                                                            ALU.mult).then_inc(bias_ready, 1)
                            if c % CPT == 1 and there(s - 2 * CPT - 1, NB * CPB):
                                i, q = 2 * j + c // CPT - 2, c // CPT
                                dve.wait_ge(exp_done, CPT * i + CPT)
                                nc.vector.tensor_reduce(rsum[:, q:q + 1], csum[:, q], AX.X, ALU.add
                                                        ).then_inc(rsum_done, 1)
                                dve.wait_ge(rsum_done, i + 1)
                                nc.vector.reciprocal(rinv[:, q:q + 1], rsum[:, q:q + 1]).then_inc(rinv_ready, 1)
                            if c % CPT == 2 and there(s - 2 * CPT - 2, NB * CPB):
                                i, q = 2 * j + c // CPT - 2, c // CPT
                                dve.wait_ge(o_lo_ready, i + 1)
                                after(dve, y_ready, i - 1)
                                nc.vector.scalar_tensor_tensor(att[:, q], ps_o3[:, q, 0:D], rinv[:, q:q + 1], o_lo[:],
                                                               ALU.mult, ALU.add).then_inc(out_read, 1)
                            if c == 1 and there(j, NB):
                                row_terms(2 * j + 1, 1)
                            if c == CPB - 2 and there(j + 1, NB):
                                row_terms(2 * j + 2, 0)
                            if c == CPB - 1 and there(j + 1, NB):
                                split_q(j + 1)

                    bodies3(dve, body)

                @block.gpsimd
                def _(pool):
                    def finish(i, par, uses):
                        a = att[:, par]
                        pool.wait_ge(out_read, i + 1)
                        nc.gpsimd.tensor_tensor(a, a, o_bias[:], ALU.add).then_inc(fin_steps, 1)
                        pool.wait_ge(fin_steps, 2 * i + 1)
                        pool.wait_ge(xg_loaded[par], 32 * uses)
                        nc.gpsimd.tensor_tensor(a, a, g_in3[:, par], ALU.mult).then_inc(fin_steps, 1)
                        pool.wait_ge(fin_steps, 2 * i + 2)
                        after(pool, y_stored[par], 16 * (uses - 1))
                        nc.gpsimd.tensor_tensor(y_out[:, par], a, x_in3[:, par], ALU.add).then_inc(y_ready, 1)

                    def body(j):
                        for p in range(2):
                            if there(2 * j - 2 + p, NT):
                                finish(2 * j - 2 + p, p, j)

                    bodies3(pool, body)


def kernel(**inputs):
    import numpy as np
    import concourse.bacc as bacc
    from concourse.bass_utils import run_bass_kernel_spmd

    def given(name):
        return np.asarray(inputs[name])

    arrays = {
        "x": given("L0_attn_x"),
        "wq": given("L0_attn_Wq"),
        "wk": given("L0_attn_Wk"),
        "wv": given("L0_attn_Wv"),
        "wo_t": given("L0_attn_Wo").T,
        "cols": np.stack([given("L0_attn_bq"), given("L0_attn_bk"), given("L0_attn_bv")], axis=1),
        "gate_t": given("L0_ffn_gate_w").T,
        "gate_b": given("L0_ffn_gate_b")[None, :],
        "expert_t": given("L0_ffn_expert_w").reshape(E * D, D).T,
        "expert_b": given("L0_ffn_expert_b"),
        "bo": given("L0_attn_bo")[None, :],
    }
    nc = bacc.Bacc("TRN2", target_bir_lowering=False, num_devices=1)
    feeds, args = {}, []
    for name, a in arrays.items():
        a = np.ascontiguousarray(a)
        feeds[f"in_{name}"] = a
        args.append(nc.dram_tensor(f"in_{name}", a.shape, mybir.dt.from_np(a.dtype), kind="ExternalInput").ap())
    out = nc.dram_tensor("out_y", [1, S, D], F32, kind="ExternalOutput").ap()
    build(nc, *args, out)
    result = run_bass_kernel_spmd(nc, [feeds], core_ids=[0])
    return result.results[0]["out_y"]
```
